# Optimizing a Trainium2 kernel written in Bass

```python
import numpy as np
import jax
import jax.numpy as jnp

def _softmax(x, axis=-1):
    return jax.nn.softmax(x, axis=axis)

def _gelu(x):
    return jax.nn.gelu(x, approximate=True)

def _silu(x):
    return jax.nn.silu(x)

def _sigmoid(x):
    return jax.nn.sigmoid(x)

def _layernorm(x, axis=-1, eps=1e-05):
    m = jnp.mean(x, axis=axis, keepdims=True)
    v = jnp.var(x, axis=axis, keepdims=True)
    return (x - m) / jnp.sqrt(v + eps)

def _scatter_add(tgt, idx, src, axis=0):
    return tgt.at[idx].add(src)

def _segment_sum(src, seg, n):
    return jax.ops.segment_sum(src, seg, n)
kernel_name = 'mk_gnn_ffn_d1_gnn_r8_7f80a8'

def setup_inputs(seed: int=0):
    np.random.seed(seed)
    _w = jnp.asarray

    def _rec_inputs():
        import jax
        import jax.numpy as jnp
        _gk = jax.random.key(seed)
        x = -0.0003713 + 1 * jax.random.normal(jax.random.fold_in(_gk, 1), (6250, 256), jnp.float32)
        src = jax.random.randint(jax.random.fold_in(_gk, 2), (200000,), 0, 6250, jnp.int32)
        dst = jax.random.randint(jax.random.fold_in(_gk, 3), (200000,), 0, 6250, jnp.int32)
        _o = jnp.argsort(dst, stable=True)
        src = src[_o]
        dst = dst[_o]
        edge_type_16 = jax.random.randint(jax.random.fold_in(_gk, 12), (200000,), 0, 16, jnp.int32)
        edge_weight1 = jax.random.uniform(jax.random.fold_in(_gk, 13), (200000, 1), jnp.float32, 0.0, 1)
        return (x, src, dst, edge_type_16, edge_weight1)
    x, src, dst, edge_type_16, edge_weight1 = _rec_inputs()

    def _L0_gnn_setup():
        import jax, jax.numpy as jnp
        import numpy as np
        N_NODES = 6250
        N_EDGES = 100000
        NUM_RELS = 16
        FEAT = 256
        OUT = 256
        key = jax.random.key(seed)
        ks = jax.random.split(key, 7)
        h = jax.random.normal(ks[0], (N_NODES, FEAT), dtype=jnp.float32)
        norm = jax.random.uniform(ks[1], (N_EDGES, 1), dtype=jnp.float32)
        weight = jax.random.normal(ks[2], (NUM_RELS, FEAT, OUT), dtype=jnp.float32) * 0.05
        gate_weight = jax.random.normal(ks[3], (NUM_RELS, FEAT, 1), dtype=jnp.float32) * 0.05
        src = jax.random.randint(ks[4], (N_EDGES,), 0, N_NODES)
        dst = jax.random.randint(ks[5], (N_EDGES,), 0, N_NODES)
        rel_type = jax.random.randint(ks[6], (N_EDGES,), 0, NUM_RELS)
        return {'h': h, 'norm': norm, 'weight': weight, 'gate_weight': gate_weight, 'src': src, 'dst': dst, 'rel_type': rel_type}
    _L0_gnn_all = _L0_gnn_setup()
    _L0_gnn_in = {k: v for k, v in _L0_gnn_all.items() if k in ('weight', 'gate_weight')}
    del _L0_gnn_all

    def _L0_ffn_setup():
        import math
        import jax, jax.numpy as jnp
        import numpy as np
        CAPACITY_FACTOR = 1.25
        key = jax.random.key(seed)
        ks = jax.random.split(key, 5)
        B, L, D, F, E = (8, 1024, 256, 1024, 8)
        h = jax.random.normal(ks[0], (B, L, D), dtype=jnp.float32)
        gate_w = jax.random.normal(ks[1], (D, E), dtype=jnp.float32) * 0.02
        gate_b = jnp.zeros((E,), dtype=jnp.float32)
        w1 = jax.random.normal(ks[2], (E, D, F), dtype=jnp.float32) * (1.0 / math.sqrt(D))
        b1 = jnp.zeros((E, F), dtype=jnp.float32)
        w2 = jax.random.normal(ks[3], (E, F, D), dtype=jnp.float32) * (1.0 / math.sqrt(F))
        b2 = jnp.zeros((E, D), dtype=jnp.float32)
        return {'h': h, 'gate_w': gate_w, 'gate_b': gate_b, 'w1': w1, 'b1': b1, 'w2': w2, 'b2': b2}
    _L0_ffn_all = _L0_ffn_setup()
    _L0_ffn_in = {k: v for k, v in _L0_ffn_all.items() if k in ('gate_w', 'gate_b', 'w1', 'b1', 'w2', 'b2')}
    del _L0_ffn_all
    return {'x': x, 'src': src, 'dst': dst, 'edge_type_16': edge_type_16, 'edge_weight1': edge_weight1, 'L0_gnn_weight': _L0_gnn_in['weight'], 'L0_gnn_gate_weight': _L0_gnn_in['gate_weight'], 'L0_ffn_gate_w': _L0_ffn_in['gate_w'], 'L0_ffn_gate_b': _L0_ffn_in['gate_b'], 'L0_ffn_w1': _L0_ffn_in['w1'], 'L0_ffn_b1': _L0_ffn_in['b1'], 'L0_ffn_w2': _L0_ffn_in['w2'], 'L0_ffn_b2': _L0_ffn_in['b2']}

def reference(x, src, dst, edge_type_16, edge_weight1, L0_gnn_weight, L0_gnn_gate_weight, L0_ffn_gate_w, L0_ffn_gate_b, L0_ffn_w1, L0_ffn_b1, L0_ffn_w2, L0_ffn_b2):
    import jax
    import jax.numpy as jnp

    def _L0_gnn_ref(h, norm, weight, gate_weight, src, dst, rel_type):
        import jax, jax.numpy as jnp
        import numpy as np
        N_NODES = 6250
        N_EDGES = 100000
        NUM_RELS = 16
        FEAT = 256
        OUT = 256
        n_nodes = h.shape[0]
        all_msg = jnp.einsum('nf,rfo->rno', h, weight)
        msg = all_msg[rel_type, src] * norm
        all_gate = jnp.einsum('nf,rf->rn', h, gate_weight[..., 0])
        gate = jax.nn.sigmoid(all_gate[rel_type, src])[:, None]
        msg = msg * gate
        agg = jax.ops.segment_sum(msg, dst, num_segments=n_nodes)
        return jax.nn.relu(agg)

    def _L0_ffn_ref(h, gate_w, gate_b, w1, b1, w2, b2):
        import math
        import jax, jax.numpy as jnp
        import numpy as np
        CAPACITY_FACTOR = 1.25
        B, L, D = h.shape
        E = gate_w.shape[1]
        T = B * L
        C = max(1, math.ceil(CAPACITY_FACTOR * T / E))
        x = h.reshape(T, D)
        logits = x @ gate_w + gate_b
        probs = jax.nn.softmax(logits, axis=-1)
        idx = jnp.argmax(probs, axis=-1)
        prb = jnp.take_along_axis(probs, idx[:, None], axis=1)[:, 0]
        one_hot = jax.nn.one_hot(idx, E, dtype=jnp.float32)
        pos = (jnp.cumsum(one_hot, axis=0) * one_hot).sum(-1).astype(jnp.int32) - 1
        kept = pos < C
        pos_safe = jnp.where(kept, pos, C)
        buf = jnp.zeros((E, C, D), dtype=h.dtype).at[idx, pos_safe].set(x, mode='drop')
        hmid = jax.nn.relu(jnp.einsum('ecd,edf->ecf', buf, w1) + b1[:, None, :])
        ybuf = jnp.einsum('ecf,efd->ecd', hmid, w2) + b2[:, None, :]
        pos_g = jnp.minimum(pos, C - 1)
        y_tok = ybuf[idx, pos_g] * (prb * kept)[:, None]
        y = y_tok.reshape(B, L, D)
        y = jnp.nan_to_num(y, nan=0.0, posinf=10000.0, neginf=-10000.0)
        return y
    x = x + _L0_gnn_ref(_layernorm(x, axis=-1), edge_weight1, L0_gnn_weight, L0_gnn_gate_weight, src, dst, edge_type_16)
    x = x + _L0_ffn_ref(_layernorm(x, axis=-1)[None], L0_ffn_gate_w, L0_ffn_gate_b, L0_ffn_w1, L0_ffn_b1, L0_ffn_w2, L0_ffn_b2)[0]
    return x

_drawn_inputs = setup_inputs


def setup_inputs(seed=0):
    import zlib

    import numpy as np

    out = dict(_drawn_inputs(seed))
    spreads = {'L0_ffn_gate_b': (0.0, 0.1), 'L0_ffn_b1': (0.0, 0.8), 'L0_ffn_b2': (0.0, 0.602)}
    factors = {}
    for name, (base, spread) in spreads.items():
        noise = np.random.default_rng([zlib.crc32(name.encode()), seed]).standard_normal(out[name].shape)
        drawn = base * np.exp(spread * noise) if base else spread * noise
        out[name] = jnp.asarray(drawn.astype(out[name].dtype))
    for name, factor in factors.items():
        out[name] = (out[name] * factor).astype(out[name].dtype)
    return out
```

```python
import concourse.bass as bass
from concourse import mybir
from contextlib import ExitStack

FP32 = mybir.dt.float32
INT32 = mybir.dt.int32
ALU = mybir.AluOpType
ACT = mybir.ActivationFunctionType
AX = mybir.AxisListType

P = 128
BANKS = 8
BANK = 512
EPS = 1e-5
FLOAT_MAX = 3.4028234663852886e38
NAN_AS, POSINF_AS, NEGINF_AS = 0.0, 10000.0, -10000.0
GROUP = 8
SETS = 4
RING = SETS * GROUP


def cdiv(a, b):
    return (a + b - 1) // b


class Shapes:

    def __init__(s, x, src, weight, w1, gate_w):
        s.N, s.D = x.shape
        s.E, = src.shape
        s.R = weight.shape[0]
        s.X = gate_w.shape[1]
        s.F = w1.shape[2]
        s.KD = s.D // P
        s.KF = s.F // P
        s.NT = cdiv(s.N, P)
        s.last = s.N - (s.NT - 1) * P
        s.T = cdiv(s.E, P)
        s.T_run = cdiv(s.T, RING) * RING
        s.EC = cdiv(s.T_run, P)
        s.T_pad = s.EC * P
        s.CAP = max(1, -(-5 * s.N // (4 * s.X)))
        s.ST = cdiv(s.CAP, P)
        s.SLOTS = s.X * s.CAP


def build(nc, x, src, dst, rel, norm, weight, gate_weight, gate_w, gate_b, w1, b1, w2, b2, out):
    s = Shapes(x, src, weight, w1, gate_w)
    N, D, R, X, F, KD, KF, NT, T = s.N, s.D, s.R, s.X, s.F, s.KD, s.KF, s.NT, s.T
    CAP, ST = s.CAP, s.ST
    with ExitStack() as ctx:
        def sb(name, shape, dt=FP32):
            return ctx.enter_context(nc.sbuf_tensor(name, shape, dt))

        def sem(name):
            return ctx.enter_context(nc.semaphore(name))

        def dram(name, shape, dt=FP32):
            return nc.dram_tensor(name, shape, dt).ap()

        m = {
            "message": dram("message_table", [N * R, D]),
            "block_scratch": dram("block_scratch", [2, s.T_pad], FP32),
            "buf": dram("expert_buf", [s.SLOTS, D]),
            "ybuf": dram("expert_out", [s.SLOTS, D]),
        }
        m["x"] = sb("x_rows", [P, NT, D])
        m["ident"] = sb("ident", [P, P])
        m["iota"] = sb("iota", [P, P])
        m["tri"] = sb("tri", [P, P])
        m["ones"] = sb("ones", [P, P])
        m["mv"] = sb("mean_var", [P, NT, 2])
        m["rstd"] = sb("rstd", [P, NT])
        m["nmr"] = sb("neg_mean_rstd", [P, NT])
        m["stats"] = sb("stats", [P, NT, 6])
        m["slot"] = sb("slot", [P, NT], INT32)
        m["share"] = sb("share", [P, NT])
        m["row_of"] = sb("row_of", [P, s.T_pad], INT32)
        m["dst_in"] = sb("dst_in", [P, s.T_pad])
        m["norm_of"] = sb("norm_of", [P, s.T_pad])
        m["group_row"] = sb("group_row", [1, s.T_pad // GROUP, 2], INT32)
        m["block_base"] = sb("block_base", [P, NT])
        m["bank"] = [ctx.enter_context(nc.psum_tensor(f"bank{i}", [P, BANK], FP32)) for i in range(BANKS)]
        tables(nc, s, m, x, src, dst, rel, norm, weight, gate_weight)
        with ExitStack() as inner:
            m["agg"] = inner.enter_context(nc.sbuf_tensor("agg", [P, NT, D], FP32))
            edges(nc, s, m)
            routing(nc, s, m, gate_w, gate_b)
        experts(nc, s, m, w1, b1, w2, b2)
        combine(nc, s, m, out)


def tables(nc, s, m, x, src, dst, rel, norm, weight, gate_weight):
    N, D, R, KD, NT, T, EC = s.N, s.D, s.R, s.KD, s.NT, s.T, s.EC
    PAIR = BANK // D
    NP = R // PAIR
    MAIN = 4
    CHUNK = 7
    NCH = cdiv(NT, CHUNK)
    with ExitStack() as ctx:
        def sb(name, shape, dt=FP32):
            return ctx.enter_context(nc.sbuf_tensor(name, shape, dt))

        def sem(name):
            return ctx.enter_context(nc.semaphore(name))

        W = sb("W", [P, KD, R, D])
        GW_rows = sb("GW_rows", [R, D])
        GW = sb("GW", [P, KD, R])
        rows = [sb(f"table_rows{i}", [P, R, D]) for i in range(2)]
        raw = {n: sb(f"raw_{n}", [P, EC, P], INT32) for n in ("src", "dst", "rel")}
        raw["norm"] = sb("raw_norm", [P, EC, P])
        dst_f = raw["dst"][:, :, :].bitcast(FP32)
        idx_f = raw["src"][:, :, :].bitcast(FP32)
        span_f = sb("span_f", [P, 2, EC])
        span_i = sb("span_i", [P, 2, EC], INT32)
        span_b = sb("span_b", [P, 2, EC])
        row_f = sb("row_f", [1, 2, s.T_pad])
        grp_f = sb("grp_f", [1, 2, s.T_pad // GROUP])
        h = [sb(f"h{i}", [P, D]) for i in range(2)]
        hT = [sb(f"hT{i}", [P, KD, P]) for i in range(2)]
        sg = [sb(f"sg{i}", [P, R]) for i in range(2)]
        bank = m["bank"]
        pT = bank[0:2]
        pG = bank[2]
        pE = bank[3]
        main = bank[4:8]

        x_loaded = [sem(f"x_loaded{c}") for c in range(NCH)]
        x_padded = sem("x_padded")
        w_loaded = sem("w_loaded")
        gw_loaded = sem("gw_loaded")
        edges_padded = sem("edges_padded")
        edges_loaded = [sem(f"edges_loaded{i}") for i in range(4)]
        consts_ready = sem("consts_ready")
        consts_step = sem("consts_step")
        dve_step = sem("dve_step")
        var_ready = sem("var_ready")
        std_ready = sem("std_ready")
        h_ready = sem("h_ready")
        hT_in_psum = sem("hT_in_psum")
        hT_ready = sem("hT_ready")
        gw_in_psum = sem("gw_in_psum")
        gw_ready = sem("gw_ready")
        gate_in_psum = sem("gate_in_psum")
        gate_ready = sem("gate_ready")
        pair_in_psum = sem("pair_in_psum")
        evac_act = sem("evac_act")
        evac_dve = sem("evac_dve")
        table_stored = [sem(f"table_stored{i}") for i in range(2)]
        spans_ready = sem("spans_ready")
        spans_stored = sem("spans_stored")
        spans_loaded = sem("spans_loaded")
        edge_cols_ready = sem("edge_cols_ready")
        edgeT_in_psum = sem("edgeT_in_psum")
        edgeT_copied = sem("edgeT_copied")
        base_ready = sem("base_ready")
        base_in_psum = sem("base_in_psum")
        base_used = sem("base_used")

        EARLY = min(8, (NT - 1) // 2 * 2)
        full_tiles = T - 1 if s.E % P else T
        spread = full_tiles // (EC - 1) if EC > 1 else 0
        spread = min(spread, P)
        head = P * (EC - 1)

        def edge_loads(sp, name, ap, k):
            flat = ap if len(ap.shape) == 1 else ap.rearrange("e o -> (e o)")
            sp.dma_start(raw[name][:, 0:EC - 1, :],
                         flat[0:head * P].rearrange("(p j e) -> p j e", j=EC - 1, e=P)).then_inc(edges_loaded[k], 16)
            n = full_tiles - head
            sp.dma_start(raw[name][0:n, EC - 1, :],
                         flat[head * P:full_tiles * P].rearrange("(p e) -> p e", e=P)).then_inc(edges_loaded[k], 16)
            if s.E % P:
                rest = s.E - full_tiles * P
                sp.dma_start(raw[name][n:n + 1, EC - 1, 0:rest],
                             flat[full_tiles * P:s.E].rearrange("(p e) -> p e", e=rest)).then_inc(edges_loaded[k], 16)

        EDGE_DMAS = 48 if s.E % P else 32

        with nc.Block() as block:
            @block.sync
            def _(sp):
                sp.wait_ge(x_padded, 1)
                for c in range(NCH):
                    a, b = c * CHUNK, min((c + 1) * CHUNK, NT)
                    if b == NT:
                        b -= 1
                        sp.dma_start(m["x"][0:s.last, NT - 1, :], x[(NT - 1) * P:N, :]).then_inc(x_loaded[c], 16)
                    if b > a:
                        sp.dma_start(m["x"][:, a:b, :],
                                     x[a * P:b * P, :].rearrange("(t p) f -> p t f", p=P)).then_inc(x_loaded[c], 16)
                    if c == 0:
                        sp.dma_start(GW_rows[:, :], gate_weight.rearrange("r d o -> r (d o)")).then_inc(gw_loaded, 16)
                        for k in range(KD):
                            sp.dma_start(W[:, k, :, :],
                                         weight[:, k * P:(k + 1) * P, :].rearrange("r p o -> p r o")).then_inc(w_loaded, 16)
                sp.wait_ge(edges_padded, 4)
                for k, (name, ap) in enumerate((("src", src), ("rel", rel), ("dst", dst), ("norm", norm))):
                    edge_loads(sp, name, ap, k)

                def store(i, par):
                    sp.wait_ge(evac_act, NP // 2 * (i + 1))
                    sp.wait_ge(evac_dve, NP // 2 * (i + 1))
                    return rows[par]

                def store_full(i, par):
                    r = store(i, par)
                    sp.dma_start(m["message"][bass.ds(i * (P * R), P * R), :].rearrange("(p r) o -> p r o", r=R),
                                 r[:, :, :]).then_inc(table_stored[par], 16)

                with sp.Fori(0, EARLY // 2) as j:
                    store_full(2 * j, 0)
                    store_full(2 * j + 1, 1)
                sp.wait_ge(spans_ready, 1)
                for q in range(2):
                    sp.dma_start(m["block_scratch"][q, 0:head].rearrange("(p j) -> p j", j=EC - 1),
                                 span_b[:, q, 0:EC - 1]).then_inc(spans_stored, 16)
                    sp.dma_start(m["block_scratch"][q, head:head + P].rearrange("(p j) -> p j", j=1),
                                 span_b[:, q, EC - 1:EC]).then_inc(spans_stored, 16)
                sp.wait_ge(spans_stored, 64)
                sp.dma_start(row_f[0:1, :, :], m["block_scratch"].rearrange("(o q) t -> o q t", o=1)).then_inc(spans_loaded, 16)
                with sp.Fori(EARLY // 2, (NT - 1) // 2) as j:
                    store_full(2 * j, 0)
                    store_full(2 * j + 1, 1)
                for i in range((NT - 1) // 2 * 2, NT):
                    r = store(i, i % 2)
                    n = P if i < NT - 1 else s.last
                    sp.dma_start(m["message"][i * P * R:(i * P + n) * R, :].rearrange("(p r) o -> p r o", r=R),
                                 r[0:n, :, :]).then_inc(table_stored[i % 2], 16)
                for par in range(2):
                    sp.wait_ge(table_stored[par], 16 * len(range(par, NT, 2)))

            @block.gpsimd
            def _(pool):
                pool.memset(m["x"][:, NT - 1, :], 0.0).then_inc(x_padded, 1)
                pool.memset(m["ident"][:, :], 0.0).then_inc(consts_step, 1)
                pool.memset(m["ones"][:, :], 1.0).then_inc(consts_step, 1)
                for name, fill in (("src", 0), ("rel", 0), ("dst", N - 1), ("norm", 0.0)):
                    pool.memset(raw[name][:, EC - 1, :], fill).then_inc(edges_padded, 1)
                pool.wait_ge(consts_step, 2)
                pool.affine_select(out=m["ident"][:, :], in_=m["ident"][:, :], compare_op=ALU.not_equal, fill=1.0,
                                   base=0, pattern=[[-1, P]], channel_multiplier=1).then_inc(consts_ready, 1)
                pool.affine_select(out=m["tri"][:, :], in_=m["ones"][:, :], compare_op=ALU.is_ge, fill=0.0,
                                   base=0, pattern=[[1, P]], channel_multiplier=-1).then_inc(consts_ready, 1)
                pool.iota(m["iota"][:, :], pattern=[[1, P]], base=0, channel_multiplier=0,
                          allow_small_or_imprecise_dtypes=True).then_inc(consts_ready, 1)
                pool.iota(m["block_base"][:, :], pattern=[[P, NT]], base=0, channel_multiplier=0,
                          allow_small_or_imprecise_dtypes=True).then_inc(consts_ready, 1)

            @block.vector
            def _(dve):
                chain = [0]

                def link(ins):
                    chain[0] += 1
                    ins.then_inc(dve_step, 1)
                    dve.wait_ge(dve_step, chain[0])

                for c in range(NCH):
                    a, b = c * CHUNK, min((c + 1) * CHUNK, NT)
                    dve.wait_ge(x_loaded[c], 16 if b < NT or b - a == 1 else 32)
                    for i in range(a, b):
                        last = nc.vector.bn_stats(m["stats"][:, i, :], m["x"][:, i, :])
                    link(last)
                    for i in range(a, b):
                        last = nc.vector.bn_aggr(m["mv"][:, i, :], m["stats"][:, i, :])
                    link(last)
                nc.vector.tensor_scalar(m["nmr"][:, :], m["mv"][:, :, 1], EPS, None, ALU.add).then_inc(var_ready, 1)
                dve.wait_ge(std_ready, 1)
                link(nc.vector.reciprocal(m["rstd"][:, :], m["nmr"][:, :]))

                def normalise(i, par):
                    if not (isinstance(i, int) and i == 0):
                        dve.wait_ge(hT_in_psum, i)
                    nc.vector.tensor_scalar(h[par][:, :], m["x"][:, bass.ds(i, 1), :].rearrange("p a f -> p (a f)"),
                                            m["mv"][:, bass.ds(i, 1), 0:1].rearrange("p a f -> p (a f)"),
                                            m["rstd"][:, bass.ds(i, 1)],
                                            ALU.subtract, ALU.mult).then_inc(h_ready, 1)

                def step(i, par, more=True, first=False):
                    if more:
                        normalise(i + 1, 1 - par)
                    if not first:
                        dve.wait_ge(table_stored[par], 16 * (i // 2) if isinstance(i, int) else 8 * i - 8 * par)
                    dve.wait_ge(gate_ready, i + 1)
                    for j in range(1, NP, 2):
                        dve.wait_ge(pair_in_psum, NP * i + j + 1)
                        for q in range(PAIR):
                            r = j * PAIR + q
                            last = nc.vector.tensor_scalar(rows[par][:, r, :], main[j % MAIN][:, q * D:(q + 1) * D],
                                                           sg[par][:, r:r + 1], None, ALU.mult)
                        last.then_inc(evac_dve, 1)

                normalise(0, 0)
                step(0, 0, first=True)
                step(1, 1, first=True)
                with dve.Fori(1, EARLY // 2) as j:
                    step(2 * j, 0)
                    step(2 * j + 1, 1)

                for k in range(4):
                    dve.wait_ge(edges_loaded[k], EDGE_DMAS)
                nc.vector.tensor_copy(dst_f[:, :, :], raw["dst"][:, :, :])
                link(nc.vector.tensor_copy(idx_f[:, :, :], raw["src"][:, :, :]))
                nc.vector.scalar_tensor_tensor(idx_f[:, :, :].rearrange("p j e -> p (j e)"),
                                               idx_f[:, :, :].rearrange("p j e -> p (j e)"), float(R),
                                               raw["rel"][:, :, :].rearrange("p j e -> p (j e)"),
                                               ALU.mult, ALU.add).then_inc(edge_cols_ready, 1)
                nc.vector.tensor_reduce(span_f[:, 0, :], dst_f[:, :, :], AX.X, ALU.min)
                link(nc.vector.tensor_reduce(span_f[:, 1, :], dst_f[:, :, :], AX.X, ALU.max))
                link(nc.vector.tensor_copy(span_i[:, :, :], span_f[:, :, :]))
                shift = P.bit_length() - 1
                link(nc.vector.tensor_scalar(span_i[:, :, :], span_i[:, :, :], shift, None, ALU.arith_shift_right))
                nc.vector.tensor_copy(span_b[:, :, :], span_i[:, :, :]).then_inc(spans_ready, 1)
                kinds = (("row_of", idx_f), ("dst_in", dst_f), ("norm_of", raw["norm"]))
                n = 0
                for name, _ in kinds:
                    to = m[name]
                    for j0 in range(0, EC, 4):
                        w = min(4, EC - j0)
                        n += 1
                        dve.wait_ge(edgeT_in_psum, n)
                        for j in range(j0, j0 + w):
                            o = to[:, 0:head].rearrange("e (p j) -> e j p", j=EC - 1)[:, j, :] if j < EC - 1 else to[:, head:head + P]
                            last = nc.vector.tensor_copy(o, pE[:, (j - j0) * P:(j - j0 + 1) * P])
                        last.then_inc(edgeT_copied, 1)
                dve.wait_ge(spans_loaded, 16)
                link(nc.vector.tensor_reduce(grp_f[0:1, 0, :], row_f[0:1, 0, :].rearrange("o (g t) -> o g t", t=GROUP), AX.X, ALU.min))
                link(nc.vector.tensor_reduce(grp_f[0:1, 1, :], row_f[0:1, 1, :].rearrange("o (g t) -> o g t", t=GROUP), AX.X, ALU.max))
                nc.vector.tensor_copy(m["group_row"][0:1, :, 0], grp_f[0:1, 0, :])
                nc.vector.tensor_tensor(m["group_row"][0:1, :, 1], grp_f[0:1, 1, :], grp_f[0:1, 0, :], ALU.subtract)
                nc.vector.tensor_scalar(row_f[0:1, 0, :].rearrange("o (g t) -> o g t", t=GROUP),
                                        grp_f[0:1, 0, :].rearrange("o (g t) -> o g t", t=1).broadcast_to([1, s.T_pad // GROUP, GROUP]),
                                        float(P), None, ALU.mult).then_inc(base_ready, 1)
                for k, c0 in enumerate(range(0, s.T_pad, BANK)):
                    c1 = min(c0 + BANK, s.T_pad)
                    dve.wait_ge(base_in_psum, k + 1)
                    nc.vector.tensor_tensor(m["dst_in"][:, c0:c1], m["dst_in"][:, c0:c1], pE[:, 0:c1 - c0],
                                            ALU.subtract).then_inc(base_used, 1)

                with dve.Fori(EARLY // 2, (NT - 1) // 2) as j:
                    step(2 * j, 0)
                    step(2 * j + 1, 1)
                for i in range((NT - 1) // 2 * 2, NT):
                    step(i, i % 2, more=i < NT - 1)

            @block.scalar
            def _(act):
                act.wait_ge(var_ready, 1)
                nc.scalar.activation(m["nmr"][:, :], m["nmr"][:, :], ACT.Sqrt).then_inc(std_ready, 1)

                def copy_hT(i, par):
                    act.wait_ge(hT_in_psum, i + 1)
                    nc.scalar.activation(hT[par][:, :, :].rearrange("p k n -> p (k n)"), pT[par][:, 0:KD * P],
                                         ACT.Copy).then_inc(hT_ready, 1)

                def step(i, par, more=True, first=False):
                    if more:
                        copy_hT(i + 1, 1 - par)
                    act.wait_ge(gate_in_psum, i + 1)
                    nc.scalar.activation(sg[par][:, :], pG[:, 0:R], ACT.Sigmoid).then_inc(gate_ready, 1)
                    act.wait_ge(gate_ready, i + 1)
                    if not first:
                        act.wait_ge(table_stored[par], 16 * (i // 2) if isinstance(i, int) else 8 * i - 8 * par)
                    for j in range(0, NP, 2):
                        act.wait_ge(pair_in_psum, NP * i + j + 1)
                        for q in range(PAIR):
                            r = j * PAIR + q
                            last = nc.scalar.activation(rows[par][:, r, :], main[j % MAIN][:, q * D:(q + 1) * D],
                                                        ACT.Copy, scale=sg[par][:, r:r + 1])
                        last.then_inc(evac_act, 1)

                act.wait_ge(gw_in_psum, 1)
                nc.scalar.activation(GW[:, :, :].rearrange("p k r -> p (k r)"), pG[:, 0:KD * R], ACT.Copy).then_inc(gw_ready, 1)
                copy_hT(0, 0)
                step(0, 0, first=True)
                step(1, 1, first=True)
                with act.Fori(1, EARLY // 2) as j:
                    step(2 * j, 0)
                    step(2 * j + 1, 1)
                with act.Fori(EARLY // 2, (NT - 1) // 2) as j:
                    step(2 * j, 0)
                    step(2 * j + 1, 1)
                for i in range((NT - 1) // 2 * 2, NT):
                    step(i, i % 2, more=i < NT - 1)

            @block.tensor
            def _(pe):
                pe.wait_ge(consts_ready, 4)

                def transposes(i, par):
                    pe.wait_ge(h_ready, i + 1)
                    if not (isinstance(i, int) and i == 0):
                        pe.wait_ge(hT_ready, i)
                    for k in range(KD):
                        last = nc.tensor.transpose(pT[par][:, k * P:(k + 1) * P], h[par][:, k * P:(k + 1) * P],
                                                   m["ident"][:, :])
                    last.then_inc(hT_in_psum, 1)

                def step(i, par, more=True, first=False):
                    if more:
                        transposes(i + 1, 1 - par)
                    pe.wait_ge(hT_ready, i + 1)
                    if not first:
                        pe.wait_ge(gate_ready, i)
                    for k in range(KD):
                        last = nc.tensor.matmul(pG[:, 0:R], hT[par][:, k, :], GW[:, k, :], start=k == 0, stop=k == KD - 1)
                    last.then_inc(gate_in_psum, 1)
                    for j in range(NP):
                        if not (first and j < MAIN):
                            pe.wait_ge(evac_dve if j % 2 else evac_act, NP // 2 * i + j // 2 - (MAIN // 2 - 1))
                        for k in range(KD):
                            last = nc.tensor.matmul(main[j % MAIN][:, :], hT[par][:, k, :],
                                                    W[:, k, j * PAIR:(j + 1) * PAIR, :].rearrange("p r o -> p (r o)"),
                                                    start=k == 0, stop=k == KD - 1)
                        last.then_inc(pair_in_psum, 1)

                transposes(0, 0)
                pe.wait_ge(gw_loaded, 16)
                for k in range(KD):
                    last = nc.tensor.transpose(pG[:, k * R:(k + 1) * R], GW_rows[:, k * P:(k + 1) * P], m["ident"][0:R, 0:R])
                last.then_inc(gw_in_psum, 1)
                pe.wait_ge(gw_ready, 1)
                pe.wait_ge(w_loaded, 16 * KD)
                step(0, 0, first=True)
                step(1, 1)
                with pe.Fori(1, EARLY // 2) as j:
                    step(2 * j, 0)
                    step(2 * j + 1, 1)

                pe.wait_ge(edge_cols_ready, 1)
                n = 0
                for of in (idx_f, dst_f, raw["norm"]):
                    for j0 in range(0, EC, 4):
                        w = min(4, EC - j0)
                        pe.wait_ge(edgeT_copied, n)
                        for j in range(j0, j0 + w):
                            last = nc.tensor.transpose(pE[:, (j - j0) * P:(j - j0 + 1) * P], of[:, j, :], m["ident"][:, :])
                        last.then_inc(edgeT_in_psum, 1)
                        n += 1
                pe.wait_ge(edgeT_copied, n)
                pe.wait_ge(base_ready, 1)
                for k, c0 in enumerate(range(0, s.T_pad, BANK)):
                    c1 = min(c0 + BANK, s.T_pad)
                    pe.wait_ge(base_used, k)
                    nc.tensor.matmul(pE[:, 0:c1 - c0], m["ones"][0:1, :], row_f[0:1, 0, c0:c1],
                                     start=True, stop=True).then_inc(base_in_psum, 1)

                with pe.Fori(EARLY // 2, (NT - 1) // 2) as j:
                    step(2 * j, 0)
                    step(2 * j + 1, 1)
                for i in range((NT - 1) // 2 * 2, NT):
                    step(i, i % 2, more=i < NT - 1)


def edges(nc, s, m):
    N, D, NT = s.N, s.D, s.NT
    ROUNDS = s.T_run // RING
    with ExitStack() as ctx:
        def sb(name, shape, dt=FP32):
            return ctx.enter_context(nc.sbuf_tensor(name, shape, dt))

        def sem(name):
            return ctx.enter_context(nc.semaphore(name))

        gathered = sb("gathered", [P, RING, D])
        index = [sb(f"index{h}", [P, GROUP], INT32) for h in range(SETS)]
        shifted = sb("shifted", [P, GROUP])
        select = [sb(f"select{i}", [P, P]) for i in range(RING)]
        sum_of = [m["bank"][h] for h in range(SETS)]
        CLEARS = 16
        zeros = sb("zeros", [P, s.SLOTS * D // P // CLEARS])

        rows_gathered = [sem(f"rows_gathered{i}") for i in range(RING)]
        index_ready = sem("index_ready")
        select_ready = sem("select_ready")
        visit_summed = sem("visit_summed")
        visit_added = sem("visit_added")
        shifted_ready = sem("shifted_ready")
        extra_ready = sem("extra_ready")
        group_done = sem("group_done")
        zeros_ready = sem("zeros_ready")
        buf_cleared = sem("buf_cleared")
        wait_passed = sem("wait_passed")
        VISITS = s.T_run // GROUP * NT

        def span(e, g):
            _, values = nc.values_load_multi_w_load_instructions(
                m["group_row"][0:1, bass.ds(g, 1), :].rearrange("o g q -> o (g q)"),
                engines=[e.engine], min_val=0, max_val=NT - 1)
            return values

        with nc.Block() as block:
            @block.sync
            def _(sp):
                sp.wait_ge(zeros_ready, 1)
                flat = m["buf"].rearrange("s d -> (s d)").rearrange("(c p n) -> c p n", c=CLEARS, p=P)
                for c in range(CLEARS):
                    sp.dma_start(flat[c], zeros[:, :]).then_inc(buf_cleared, 16)
                sp.wait_ge(buf_cleared, 16 * CLEARS)

            @block.gpsimd
            def _(pool):
                def gather_round(b, again):
                    for h in range(SETS):
                        if again:
                            pool.wait_ge(group_done, SETS * b - SETS + h + 1)
                        pool.wait_ge(index_ready, SETS * b + h + 1)
                        pool.sem_inc(wait_passed, 1)
                        for t in range(GROUP):
                            nc.gpsimd.indirect_dma_start(
                                gathered[:, h * GROUP + t, :], None, m["message"],
                                bass.IndirectOffsetOnAxis(ap=index[h][:, t:t + 1], axis=0)
                            ).then_inc(rows_gathered[h * GROUP + t], 16)

                gather_round(0, False)
                with pool.Fori(1, ROUNDS) as b:
                    gather_round(b, True)

            @block.vector
            def _(dve):
                def prepare(g, h):
                    nc.vector.tensor_copy(index[h][:, :], m["row_of"][:, bass.ds(g * GROUP, GROUP)]).then_inc(index_ready, 1)
                    for t in range(GROUP):
                        col = g * GROUP + t
                        nc.vector.tensor_scalar(select[h * GROUP + t][:, :], m["iota"][:, :],
                                                m["dst_in"][:, bass.ds(col, 1)], m["norm_of"][:, bass.ds(col, 1)],
                                                ALU.is_equal, ALU.mult).then_inc(select_ready, 1)

                visits = dve.alloc_register("dve_visits")
                dve.reg_mov(visits, 0)
                extras = dve.alloc_register("dve_extras")
                dve.reg_mov(extras, 0)

                def add(n, block_of, h):
                    dve.wait_ge(visit_summed, n + 1)
                    dve.wait_ge(visit_added, n + 1)
                    to = m["agg"][:, bass.ds(block_of, 1), :].rearrange("p a f -> p (a f)")
                    nc.vector.tensor_tensor(to, to, sum_of[h][:, 0:D], ALU.add).then_inc(visit_added, 1)
                    dve.reg_add(visits, visits, 1)

                def add_group(g, h):
                    block0, beyond = span(dve, g)
                    n = dve.snap(visits, min_val=0, max_val=VISITS)
                    add(n, block0, h)
                    with dve.If(beyond == 0):
                        dve.nop()
                    with dve.Else():
                        with dve.Fori(0, beyond) as v:
                            n = dve.snap(visits, min_val=1, max_val=VISITS)
                            dve.reg_add(extras, extras, 1)
                            extra = dve.snap(extras, min_val=1, max_val=VISITS)
                            nc.vector.tensor_scalar(shifted[:, :], m["dst_in"][:, bass.ds(g * GROUP, GROUP)],
                                                    m["block_base"][:, bass.ds(v + 1, 1)], None,
                                                    ALU.subtract).then_inc(shifted_ready, 1)
                            dve.wait_ge(shifted_ready, extra)
                            for t in range(GROUP):
                                nc.vector.tensor_scalar(select[h * GROUP + t][:, :], m["iota"][:, :],
                                                        shifted[:, t:t + 1], m["norm_of"][:, bass.ds(g * GROUP + t, 1)],
                                                        ALU.is_equal, ALU.mult)
                            dve.drain().then_inc(extra_ready, 1)
                            at = nc.s_assert_within(block0 + v + 1, 0, NT - 1, skip_runtime_bounds_check_because=
                                                    "block0 + beyond is the last block of the group")
                            add(n, at, h)
                    dve.sem_inc(group_done, 1)

                for h in range(SETS):
                    prepare(h, h)
                nc.vector.memset(zeros[:, :], 0.0).then_inc(zeros_ready, 1)
                nc.vector.memset(m["agg"][:, :, :], 0.0).then_inc(visit_added, 1)
                with dve.Fori(0, ROUNDS - 1) as b:
                    for h in range(SETS):
                        add_group(b * SETS + h, h)
                        prepare(b * SETS + SETS + h, h)
                for h in range(SETS):
                    add_group((ROUNDS - 1) * SETS + h, h)

            @block.tensor
            def _(pe):
                visits = pe.alloc_register("pe_visits")
                pe.reg_mov(visits, 0)
                extras = pe.alloc_register("pe_extras")
                pe.reg_mov(extras, 0)

                def sum_group(b, h):
                    g = b * SETS + h
                    _, beyond = span(pe, g)
                    for t in range(GROUP):
                        slot = h * GROUP + t
                        pe.wait_ge(rows_gathered[slot], 16 * b + 16)
                        pe.wait_ge(select_ready, g * GROUP + t + 1)
                        last = nc.tensor.matmul(sum_of[h][:, 0:D], select[slot][:, :], gathered[:, slot, :],
                                                start=t == 0, stop=t == GROUP - 1)
                    last.then_inc(visit_summed, 1)
                    pe.reg_add(visits, visits, 1)
                    with pe.If(beyond == 0):
                        pe.nop()
                    with pe.Else():
                        with pe.Fori(0, beyond) as v:
                            n = pe.snap(visits, min_val=1, max_val=VISITS)
                            pe.wait_ge(visit_added, n + 1)
                            pe.reg_add(extras, extras, 1)
                            pe.wait_ge(extra_ready, pe.snap(extras, min_val=1, max_val=VISITS))
                            for t in range(GROUP):
                                last = nc.tensor.matmul(sum_of[h][:, 0:D], select[h * GROUP + t][:, :],
                                                        gathered[:, h * GROUP + t, :], start=t == 0, stop=t == GROUP - 1)
                            last.then_inc(visit_summed, 1)
                            pe.reg_add(visits, visits, 1)

                with pe.Fori(0, ROUNDS) as b:
                    for h in range(SETS):
                        sum_group(b, h)


def routing(nc, s, m, gate_w, gate_b):
    N, D, X, KD, NT, CAP = s.N, s.D, s.X, s.KD, s.NT, s.CAP
    CHUNK = 7
    NCH = cdiv(NT, CHUNK)
    m_slot, m_share = m["slot"], m["share"]
    with ExitStack() as ctx:
        def sb(name, shape, dt=FP32):
            return ctx.enter_context(nc.sbuf_tensor(name, shape, dt))

        def sem(name):
            return ctx.enter_context(nc.semaphore(name))

        h2 = m["agg"]
        hT = [sb(f"h2T{i}", [P, KD, P]) for i in range(2)]
        GW = sb("router_w", [P, KD, X])
        GB = sb("router_b", [P, X])
        L = sb("logits", [P, NT, X])
        Pe = sb("gate_exp", [P, NT, X])
        hot = sb("hot", [P, NT, X])
        tot = [sb(f"tot{i}", [P, NT, X]) for i in range(2)]
        eid = sb("expert_ids", [P, X])
        top = sb("top", [P, NT])
        den = sb("den", [P, NT])
        which = sb("which", [P, NT])
        pos = sb("pos", [P, NT])
        kept = sb("kept", [P, NT])
        slot_f = sb("slot_f", [P, NT])
        put = sb("put", [P, NT], INT32)
        token = sb("token", [P, NT])
        bank = m["bank"]
        pT = bank[0:2]
        pL, pCum, pTot = bank[2], bank[3], bank[4]

        gw_loaded = sem("router_w_loaded")
        ids_ready = sem("ids_ready")
        x2_ready = sem("x2_ready")
        step_done = sem("route_step")
        var_ready = sem("var2_ready")
        std_ready = sem("std2_ready")
        h2_ready = sem("h2_ready")
        hT_in_psum = sem("h2T_in_psum")
        hT_ready = sem("h2T_ready")
        logits_in_psum = sem("logits_in_psum")
        centred = sem("centred")
        exp_ready = sem("exp_ready")
        hot_ready = sem("hot_ready")
        counts_in_psum = sem("counts_in_psum")
        put_ready = sem("put_ready")
        scattered = sem("scattered")

        with nc.Block() as block:
            @block.sync
            def _(sp):
                sp.dma_start(GW[:, :, :], gate_w.rearrange("(k p) e -> p k e", p=P)).then_inc(gw_loaded, 16)
                sp.dma_start(GB[:, :], gate_b.rearrange("(o e) -> o e", o=1).broadcast_to([P, X])).then_inc(gw_loaded, 16)
                sp.wait_ge(gw_loaded, 32)

            @block.gpsimd
            def _(pool):
                pool.iota(eid[:, :], pattern=[[1, X]], base=0, channel_multiplier=0,
                          allow_small_or_imprecise_dtypes=True).then_inc(ids_ready, 1)
                pool.iota(token[:, :], pattern=[[P, NT]], base=0, channel_multiplier=1,
                          allow_small_or_imprecise_dtypes=True).then_inc(ids_ready, 1)
                pool.wait_ge(put_ready, 1)
                pool.wait_ge(h2_ready, NT)
                for i in range(NT):
                    nc.gpsimd.indirect_dma_start(
                        m["buf"], bass.IndirectOffsetOnAxis(ap=put[:, i:i + 1], axis=0), h2[:, i, :], None,
                        bounds_check=s.SLOTS - 1, oob_is_err=False).then_inc(scattered, 16)
                pool.wait_ge(scattered, 16 * NT)

            @block.vector
            def _(dve):
                chain = [0]

                def link(ins):
                    chain[0] += 1
                    ins.then_inc(step_done, 1)
                    dve.wait_ge(step_done, chain[0])

                for c in range(NCH):
                    a, b = c * CHUNK, min((c + 1) * CHUNK, NT)
                    link(nc.vector.scalar_tensor_tensor(
                        m["x"][:, a:b, :].rearrange("p t f -> p (t f)"), m["agg"][:, a:b, :].rearrange("p t f -> p (t f)"), 0.0,
                        m["x"][:, a:b, :].rearrange("p t f -> p (t f)"), ALU.max, ALU.add))
                    for i in range(a, b):
                        last = nc.vector.bn_stats(m["stats"][:, i, :], m["x"][:, i, :])
                    link(last)
                    for i in range(a, b):
                        last = nc.vector.bn_aggr(m["mv"][:, i, :], m["stats"][:, i, :])
                    link(last)
                    nc.vector.tensor_scalar(m["nmr"][:, a:b], m["mv"][:, a:b, 1], EPS, None, ALU.add).then_inc(var_ready, 1)
                    dve.wait_ge(std_ready, c + 1)
                    link(nc.vector.reciprocal(m["rstd"][:, a:b], m["nmr"][:, a:b]))
                    for i in range(a, b):
                        nc.vector.tensor_scalar(h2[:, i, :], m["x"][:, i, :], m["mv"][:, i, 0:1], m["rstd"][:, i:i + 1],
                                                ALU.subtract, ALU.mult).then_inc(h2_ready, 1)

                def rows3(ap):
                    return ap.rearrange("p (t o) -> p t o", o=1).broadcast_to([P, NT, X])

                dve.wait_ge(gw_loaded, 32)
                dve.wait_ge(logits_in_psum, NT)
                dve.wait_ge(ids_ready, 2)
                link(nc.vector.tensor_tensor(L[:, :, :], pL[:, 0:NT * X].rearrange("p (t e) -> p t e", e=X),
                                             GB[:, :].rearrange("p (o e) -> p o e", o=1).broadcast_to([P, NT, X]), ALU.add))
                link(nc.vector.tensor_reduce(top[:, :], L[:, :, :], AX.X, ALU.max))
                nc.vector.tensor_tensor(L[:, :, :], L[:, :, :], rows3(top[:, :]), ALU.subtract).then_inc(centred, 1)
                dve.wait_ge(exp_ready, 1)
                nc.vector.tensor_reduce(den[:, :], Pe[:, :, :], AX.X, ALU.add)
                link(nc.vector.tensor_reduce(top[:, :], Pe[:, :, :], AX.X, ALU.max))
                link(nc.vector.tensor_tensor(hot[:, :, :], Pe[:, :, :], rows3(top[:, :]), ALU.is_equal))
                link(nc.vector.reciprocal(den[:, :], den[:, :]))
                nc.vector.tensor_tensor(m_share[:, :], top[:, :], den[:, :], ALU.mult)
                e3 = eid[:, :].rearrange("p (o e) -> p o e", o=1).broadcast_to([P, NT, X])
                link(nc.vector.tensor_scalar(hot[:, :, :], hot[:, :, :], -float(X), float(X), ALU.mult, ALU.add))
                link(nc.vector.tensor_tensor(hot[:, :, :], hot[:, :, :], e3, ALU.add))
                link(nc.vector.tensor_reduce(which[:, :], hot[:, :, :], AX.X, ALU.min))
                nc.vector.tensor_tensor(hot[:, :, :], e3, rows3(which[:, :]), ALU.is_equal).then_inc(hot_ready, 1)
                dve.wait_ge(counts_in_psum, 1)
                link(nc.vector.memset(tot[0][:, 0, :], 0.0))
                link(nc.vector.tensor_copy(tot[0][:, 1:NT, :], pTot[:, 0:(NT - 1) * X].rearrange("p (t e) -> p t e", e=X)))
                a, b, w = tot[0], tot[1], 1
                while w < NT:
                    nc.vector.tensor_copy(b[:, 0:w, :], a[:, 0:w, :])
                    link(nc.vector.tensor_tensor(b[:, w:NT, :], a[:, w:NT, :], a[:, 0:NT - w, :], ALU.add))
                    a, b, w = b, a, 2 * w
                link(nc.vector.tensor_tensor(b[:, :, :], a[:, :, :], pCum[:, 0:NT * X].rearrange("p (t e) -> p t e", e=X), ALU.add))
                link(nc.vector.tensor_tensor(b[:, :, :], b[:, :, :], hot[:, :, :], ALU.mult))
                link(nc.vector.tensor_reduce(pos[:, :], b[:, :, :], AX.X, ALU.add))
                link(nc.vector.tensor_scalar(pos[:, :], pos[:, :], -1.0, None, ALU.add))
                nc.vector.tensor_scalar(kept[:, :], pos[:, :], float(CAP), None, ALU.is_lt)
                nc.vector.tensor_scalar(token[:, :], token[:, :], float(N), None, ALU.is_lt)
                link(nc.vector.tensor_scalar(pos[:, :], pos[:, :], float(CAP - 1), 0.0, ALU.min, ALU.max))
                link(nc.vector.scalar_tensor_tensor(slot_f[:, :], which[:, :], float(CAP), pos[:, :], ALU.mult, ALU.add))
                nc.vector.tensor_copy(m_slot[:, :], slot_f[:, :])
                link(nc.vector.tensor_tensor(m_share[:, :], m_share[:, :], kept[:, :], ALU.mult))
                link(nc.vector.tensor_tensor(kept[:, :], kept[:, :], token[:, :], ALU.mult))
                link(nc.vector.tensor_scalar(kept[:, :], kept[:, :], -float(s.SLOTS), float(s.SLOTS), ALU.mult, ALU.add))
                link(nc.vector.tensor_tensor(slot_f[:, :], slot_f[:, :], kept[:, :], ALU.add))
                nc.vector.tensor_copy(put[:, :], slot_f[:, :]).then_inc(put_ready, 1)

            @block.scalar
            def _(act):
                for c in range(NCH):
                    a, b = c * CHUNK, min((c + 1) * CHUNK, NT)
                    act.wait_ge(var_ready, c + 1)
                    nc.scalar.activation(m["nmr"][:, a:b], m["nmr"][:, a:b], ACT.Sqrt).then_inc(std_ready, 1)
                    for i in range(a, b):
                        act.wait_ge(hT_in_psum, i + 1)
                        nc.scalar.activation(hT[i % 2][:, :, :].rearrange("p k n -> p (k n)"), pT[i % 2][:, 0:KD * P],
                                             ACT.Copy).then_inc(hT_ready, 1)
                act.wait_ge(centred, 1)
                nc.scalar.activation(Pe[:, :, :].rearrange("p t e -> p (t e)"), L[:, :, :].rearrange("p t e -> p (t e)"),
                                     ACT.Exp).then_inc(exp_ready, 1)

            @block.tensor
            def _(pe):
                pe.wait_ge(gw_loaded, 32)

                def transposes(i):
                    pe.wait_ge(h2_ready, i + 1)
                    if i >= 1:
                        pe.wait_ge(hT_ready, i)
                    for k in range(KD):
                        last = nc.tensor.transpose(pT[i % 2][:, k * P:(k + 1) * P], h2[:, i, k * P:(k + 1) * P], m["ident"][:, :])
                    last.then_inc(hT_in_psum, 1)

                transposes(0)
                for i in range(NT):
                    if i + 1 < NT:
                        transposes(i + 1)
                    pe.wait_ge(hT_ready, i + 1)
                    for k in range(KD):
                        last = nc.tensor.matmul(pL[:, i * X:(i + 1) * X], hT[i % 2][:, k, :], GW[:, k, :],
                                                start=k == 0, stop=k == KD - 1)
                    last.then_inc(logits_in_psum, 1)
                pe.wait_ge(hot_ready, 1)
                flat = hot[:, :, :].rearrange("p t e -> p (t e)")
                nc.tensor.matmul(pCum[:, 0:NT * X], m["tri"][:, :], flat, start=True, stop=True)
                nc.tensor.matmul(pTot[:, 0:NT * X], m["ones"][:, :], flat, start=True, stop=True).then_inc(counts_in_psum, 1)


def experts(nc, s, m, w1, b1, w2, b2):
    D, X, F, KD, KF, CAP, ST = s.D, s.X, s.F, s.KD, s.KF, s.CAP, s.ST
    PER = BANK // P
    PARTS = cdiv(ST, PER)
    counts = [min(PER, ST - p * PER) for p in range(PARTS)]
    widths = [min(PER * P, CAP - p * PER * P) for p in range(PARTS)]
    with ExitStack() as ctx:
        def sb(name, shape, dt=FP32):
            return ctx.enter_context(nc.sbuf_tensor(name, shape, dt))

        def sem(name):
            return ctx.enter_context(nc.semaphore(name))

        W1 = [sb(f"w1_{i}", [P, KD, F]) for i in range(2)]
        W2 = [sb(f"w2_{i}", [P, KF, D]) for i in range(2)]
        B1 = sb("b1_rows", [X * KF, P])
        B1T = sb("b1_cols", [P, X * KF])
        b1_of = [sb(f"b1_of{i}", [P, KF]) for i in range(2)]
        B2 = sb("b2_all", [P, X, D])
        rows = [sb(f"slots{i}", [P, ST, D]) for i in range(2)]
        hT = [sb(f"slotsT{i}", [P, KD, PER * P]) for i in range(2)]
        mid = [sb(f"hidden{i}", [P, KF, PER * P]) for i in range(2)]
        y = [sb(f"y{i}", [P, PER, D]) for i in range(2)]
        bank = m["bank"]
        pT = bank[0:2]
        pH = bank[2:6]
        pY = bank[6:8]
        pB = bank[7]
        NH, NY = len(pH), len(pY)

        w_loaded = [sem(f"expert_w_loaded{i}") for i in range(2)]
        rows_loaded = [sem(f"slots_loaded{i}") for i in range(2)]
        b_loaded = sem("b_loaded")
        b1_in_psum = sem("b1_in_psum")
        b1_ready = sem("b1_ready")
        b1_of_ready = sem("b1_of_ready")
        T_in_psum = sem("slotsT_in_psum")
        T_ready = sem("slotsT_ready")
        hid_in_psum = sem("hidden_in_psum")
        hid_ready = sem("hidden_ready")
        y_in_psum = sem("y_in_psum")
        y_ready = sem("y_ready")
        expert_read = sem("expert_read")
        y_stored = [sem(f"y_stored{i}") for i in range(2)]
        TILES = sum(counts)
        PAIRS = X // 2

        turns = [(q, p) for q in range(2) for p in range(PARTS)]
        NTURN = len(turns)
        before = [sum(counts[p] for _, p in turns[:k]) for k in range(NTURN + 1)]

        def tile_rows(p, t):
            return min(P, CAP - (p * PER + t) * P)

        with nc.Block() as block:
            @block.sync
            def _(sp):
                sp.dma_start(B1[:, :], b1.rearrange("e (m p) -> (e m) p", p=P)).then_inc(b_loaded, 16)
                sp.dma_start(B2[:, :, :].rearrange("p e d -> p (e d)"),
                             b2.rearrange("e d -> (e d)").rearrange("(o n) -> o n", o=1).broadcast_to([P, X * D])).then_inc(b_loaded, 16)
                full = CAP // P
                rest = CAP - full * P

                def load(r, q):
                    e = 2 * r + q
                    base = e * CAP
                    sp.dma_start(rows[q][:, 0:full, :],
                                 m["buf"][bass.ds(base, full * P), :].rearrange("(t p) d -> p t d", p=P)).then_inc(rows_loaded[q], 16)
                    if rest:
                        sp.dma_start(rows[q][0:rest, full, :],
                                     m["buf"][bass.ds(base + full * P, rest), :]).then_inc(rows_loaded[q], 16)
                    sp.dma_start(W1[q][:, :, :], w1[bass.ds(e, 1), :, :].rearrange("e (k p) f -> p (e k) f", p=P)).then_inc(w_loaded[q], 16)
                    sp.dma_start(W2[q][:, :, :], w2[bass.ds(e, 1), :, :].rearrange("e (k p) d -> p (e k) d", p=P)).then_inc(w_loaded[q], 16)

                def store(r, k):
                    q, p = turns[k]
                    sp.wait_ge(y_ready, r * before[NTURN] + before[k + 1])
                    base = (2 * r + q) * CAP + p * PER * P
                    whole = counts[p] - (1 if widths[p] % P else 0)
                    if whole:
                        sp.dma_start(m["ybuf"][bass.ds(base, whole * P), :].rearrange("(t p) d -> p t d", p=P),
                                     y[k % 2][:, 0:whole, :]).then_inc(y_stored[k % 2], 16)
                    if widths[p] % P:
                        sp.dma_start(m["ybuf"][bass.ds(base + whole * P, widths[p] % P), :],
                                     y[k % 2][0:widths[p] % P, whole, :]).then_inc(y_stored[k % 2], 16)

                load(0, 0)
                load(0, 1)
                with sp.Fori(0, PAIRS - 1) as r:
                    for k, (q, p) in enumerate(turns):
                        store(r, k)
                        if p == PARTS - 1:
                            sp.wait_ge(expert_read, 2 * r + q + 1)
                            load(r + 1, q)
                for k in range(NTURN):
                    store(PAIRS - 1, k)
                for par in range(2):
                    per_round = sum(16 * ((counts[turns[k][1]] - (1 if widths[turns[k][1]] % P else 0) > 0) + (widths[turns[k][1]] % P > 0))
                                    for k in range(par, NTURN, 2))
                    sp.wait_ge(y_stored[par], PAIRS * per_round)

            def stores_before(k):
                return sum(16 * ((counts[turns[j][1]] - (1 if widths[turns[j][1]] % P else 0) > 0) + (widths[turns[j][1]] % P > 0))
                           for j in range(k % 2, k, 2))

            round_stores = [stores_before(NTURN + par) for par in range(2)]

            @block.scalar
            def _(act):
                act.wait_ge(b1_in_psum, 1)
                nc.scalar.activation(B1T[:, :], pB[:, 0:X * KF], ACT.Copy).then_inc(b1_ready, 1)
                act.wait_ge(b1_ready, 1)

                def hidden(r, k):
                    q, p = turns[k]
                    if p == 0:
                        nc.scalar.activation(b1_of[q][:, :], B1T[:, bass.ds((2 * r + q) * KF, KF)], ACT.Copy).then_inc(b1_of_ready, 1)
                        act.wait_ge(b1_of_ready, 2 * r + q + 1)
                    for f in range(KF):
                        act.wait_ge(hid_in_psum, (r * NTURN + k) * KF + f + 1)
                        nc.scalar.activation(mid[k % 2][:, f, 0:widths[p]], pH[f % NH][:, 0:widths[p]], ACT.Relu,
                                             bias=b1_of[q][:, f:f + 1]).then_inc(hid_ready, 1)

                with act.Fori(0, PAIRS) as r:
                    for k in range(NTURN):
                        hidden(r, k)

            @block.vector
            def _(dve):
                dve.wait_ge(b_loaded, 32)

                def columns(r, k):
                    q, p = turns[k]
                    dve.wait_ge(T_in_psum, r * NTURN + k + 1)
                    for f in range(KD):
                        last = nc.vector.tensor_copy(hT[k % 2][:, f, 0:widths[p]], pT[f][:, 0:widths[p]])
                    last.then_inc(T_ready, 1)

                def outputs(r, k, first=False):
                    q, p = turns[k]
                    if not (first and k < 2):
                        dve.wait_ge(y_stored[k % 2], r * round_stores[k % 2] + stores_before(k))
                    for t in range(counts[p]):
                        n = tile_rows(p, t)
                        dve.wait_ge(y_in_psum, r * before[NTURN] + before[k] + t + 1)
                        nc.vector.tensor_tensor(y[k % 2][0:n, t, :], pY[(before[k] + t) % NY][0:n, 0:D],
                                                B2[0:n, bass.ds(2 * r + q, 1), :].rearrange("p e d -> p (e d)"),
                                                ALU.add).then_inc(y_ready, 1)

                columns(0, 0)
                for k in range(NTURN):
                    columns((k + 1) // NTURN, (k + 1) % NTURN)
                    outputs(0, k, first=True)
                with dve.Fori(1, PAIRS - 1) as r:
                    for k in range(NTURN):
                        columns(r + (k + 1) // NTURN, (k + 1) % NTURN)
                        outputs(r, k)
                for k in range(NTURN):
                    if k + 1 < NTURN:
                        columns(PAIRS - 1, k + 1)
                    outputs(PAIRS - 1, k)

            @block.tensor
            def _(pe):
                pe.wait_ge(b_loaded, 32)
                nc.tensor.transpose(pB[:, 0:X * KF], B1[:, :], m["ident"][0:X * KF, 0:X * KF]).then_inc(b1_in_psum, 1)
                assert before[NTURN] % NY == 0 and KF % NH == 0

                def transposes(r, k):
                    q, p = turns[k]
                    if p == 0:
                        pe.wait_ge(rows_loaded[q], (r + 1) * (32 if CAP % P else 16))
                    if not (isinstance(r, int) and r == 0 and k == 0):
                        pe.wait_ge(T_ready, r * NTURN + k)
                    for t in range(counts[p]):
                        n = tile_rows(p, t)
                        for f in range(KD):
                            last = nc.tensor.transpose(pT[f][:, t * P:t * P + n],
                                                       rows[q][0:n, p * PER + t, f * P:(f + 1) * P], m["ident"][0:n, 0:n])
                    last.then_inc(T_in_psum, 1)

                def layer1(r, k, first):
                    q, p = turns[k]
                    pe.wait_ge(T_ready, r * NTURN + k + 1)
                    if p == 0:
                        pe.wait_ge(w_loaded[q], 32 * r + 32)
                    for f in range(KF):
                        if not (first and f < NH):
                            pe.wait_ge(hid_ready, (r * NTURN + k) * KF + f - (NH - 1))
                        for c in range(KD):
                            last = nc.tensor.matmul(pH[f % NH][:, 0:widths[p]], W1[q][:, c, f * P:(f + 1) * P],
                                                    hT[k % 2][:, c, 0:widths[p]], start=c == 0, stop=c == KD - 1)
                        last.then_inc(hid_in_psum, 1)

                def layer2(r, k, first):
                    q, p = turns[k]
                    for t in range(counts[p]):
                        n = tile_rows(p, t)
                        if not (first and t < NY):
                            pe.wait_ge(y_ready, r * before[NTURN] + before[k] + t - (NY - 1))
                        for f in range(KF):
                            if t == 0:
                                pe.wait_ge(hid_ready, (r * NTURN + k) * KF + f + 1)
                            last = nc.tensor.matmul(pY[(before[k] + t) % NY][0:n, 0:D], mid[k % 2][:, f, t * P:t * P + n],
                                                    W2[q][:, f, :], start=f == 0, stop=f == KF - 1)
                        last.then_inc(y_in_psum, 1)
                    if p == PARTS - 1:
                        pe.drain().then_inc(expert_read, 1)

                def turn(r, k, first=False, last=False):
                    if not last:
                        transposes(r + (k + 1) // NTURN, (k + 1) % NTURN)
                    layer1(r, k, first)
                    layer2(r, k, first)

                transposes(0, 0)
                for k in range(NTURN):
                    turn(0, k, first=k == 0)
                with pe.Fori(1, PAIRS - 1) as r:
                    for k in range(NTURN):
                        turn(r, k)
                for k in range(NTURN):
                    turn(PAIRS - 1, k, last=k == NTURN - 1)


def combine(nc, s, m, out):
    N, D, NT = s.N, s.D, s.NT
    RY = 16
    CHUNK = 7
    NCH = cdiv(NT, CHUNK)
    with ExitStack() as ctx:
        def sb(name, shape, dt=FP32):
            return ctx.enter_context(nc.sbuf_tensor(name, shape, dt))

        def sem(name):
            return ctx.enter_context(nc.semaphore(name))

        y = [sb(f"y_rows{i}", [P, D]) for i in range(RY)]
        res = sb("result", [P, NT, D])
        row_sum = sb("row_sum", [P, NT])
        flag = sb("flag", [P, 1])
        flag_row = sb("flag_row", [1, 1])
        flag_int = sb("flag_int", [1, 1], INT32)
        slot1 = sb("slot1", [P, 1], INT32)
        y1 = sb("clean_y", [P, D])
        t1 = sb("clean_t", [P, D])
        mask = sb("mask", [P, D], INT32)
        fills = {v: sb(f"fill{i}", [P, D]) for i, v in enumerate((NAN_AS, POSINF_AS, NEGINF_AS))}
        pF = m["bank"][0]

        gathered = [sem(f"y_gathered{i}") for i in range(RY)]
        res_ready = sem("res_ready")
        stored = [sem(f"out_stored{c}") for c in range(NCH)]
        step_done = sem("combine_step")
        flag_ready = sem("flag_ready")
        flag_in_psum = sem("flag_in_psum")
        flag_loaded = sem("flag_loaded")
        with nc.Block() as block:
            @block.gpsimd
            def _(pool):
                for i in range(NT):
                    if i >= RY:
                        pool.wait_ge(res_ready, i - RY + 1)
                    nc.gpsimd.indirect_dma_start(y[i % RY][:, :], None, m["ybuf"],
                                                 bass.IndirectOffsetOnAxis(ap=m["slot"][:, i:i + 1], axis=0)
                                                 ).then_inc(gathered[i % RY], 16)

            @block.vector
            def _(dve):
                for i in range(NT):
                    dve.wait_ge(gathered[i % RY], 16 * (i // RY + 1))
                    nc.vector.scalar_tensor_tensor(res[:, i, :], y[i % RY][:, :], m["share"][:, i:i + 1], m["x"][:, i, :],
                                                   ALU.mult, ALU.add, accum_out=row_sum[:, i:i + 1]).then_inc(res_ready, 1)
                dve.wait_ge(res_ready, NT)
                nc.vector.tensor_scalar(row_sum[:, :], row_sum[:, :], 0.0, 0.0, ALU.mult, ALU.is_equal).then_inc(step_done, 1)
                dve.wait_ge(step_done, 1)
                nc.vector.tensor_reduce(flag[:, :], row_sum[:, :], AX.X, ALU.min).then_inc(flag_ready, 1)
                dve.wait_ge(flag_in_psum, 1)
                nc.vector.tensor_reduce(flag_row[0:1, :], pF[0:1, 0:P], AX.X, ALU.min).then_inc(step_done, 1)
                dve.wait_ge(step_done, 2)
                nc.vector.tensor_copy(flag_int[0:1, :], flag_row[0:1, :]).then_inc(flag_loaded, 1)

            @block.tensor
            def _(pe):
                pe.wait_ge(flag_ready, 1)
                nc.tensor.transpose(pF[0:1, 0:P], flag[:, :], m["ident"][:, :]).then_inc(flag_in_psum, 1)

            @block.sync
            def _(sp):
                for c in range(NCH):
                    a, b = c * CHUNK, min((c + 1) * CHUNK, NT)
                    sp.wait_ge(res_ready, b)
                    if b == NT:
                        b -= 1
                        sp.dma_start(out[(NT - 1) * P:N, :], res[0:s.last, NT - 1, :]).then_inc(stored[c], 16)
                    if b > a:
                        sp.dma_start(out[a * P:b * P, :].rearrange("(t p) f -> p t f", p=P), res[:, a:b, :]).then_inc(stored[c], 16)
                for c in range(NCH):
                    a, b = c * CHUNK, min((c + 1) * CHUNK, NT)
                    sp.wait_ge(stored[c], 16 if b < NT or b - a == 1 else 32)
                sp.wait_ge(flag_loaded, 1)

        clean_step = sem("clean_step")
        clean_filled = sem("clean_filled")
        clean_index = sem("clean_index")
        clean_gathered = sem("clean_gathered")
        clean_ready = sem("clean_ready")
        clean_stored = sem("clean_stored")
        wait_passed = sem("clean_wait_passed")
        with nc.Block() as block:
            def finite(e):
                return nc.values_load(flag_int[0:1, 0:1], engines=[e.engine], min_val=0, max_val=1)

            @block.gpsimd
            def _(pool):
                with pool.If(finite(pool) == 0):
                    with pool.Fori(0, NT) as i:
                        pool.wait_ge(clean_index, i + 1)
                        pool.sem_inc(wait_passed, 1)
                        nc.gpsimd.indirect_dma_start(y1[:, :], None, m["ybuf"],
                                                     bass.IndirectOffsetOnAxis(ap=slot1[:, :], axis=0)).then_inc(clean_gathered, 16)
                with pool.Else():
                    pool.nop()

            @block.vector
            def _(dve):
                with dve.If(finite(dve) == 0):
                    for v, f in fills.items():
                        nc.vector.memset(f[:, :], v).then_inc(clean_filled, 1)
                    dve.wait_ge(clean_filled, 3)
                    with dve.Fori(0, NT) as i:
                        STEPS = 7
                        count = [0]

                        def link(ins):
                            count[0] += 1
                            ins.then_inc(clean_step, 1)
                            dve.wait_ge(clean_step, i * STEPS + count[0])
                            dve.sem_inc(wait_passed, 1)

                        nc.vector.tensor_copy(slot1[:, :], m["slot"][:, bass.ds(i, 1)]).then_inc(clean_index, 1)
                        dve.wait_ge(clean_gathered, i * 16 + 16)
                        link(nc.vector.tensor_scalar(t1[:, :], y1[:, :], m["share"][:, bass.ds(i, 1)], None, ALU.mult))
                        link(nc.vector.tensor_tensor(mask[:, :], t1[:, :], t1[:, :], ALU.not_equal))
                        link(nc.vector.copy_predicated(t1[:, :], mask[:, :], fills[NAN_AS][:, :]))
                        link(nc.vector.tensor_scalar(mask[:, :], t1[:, :], FLOAT_MAX, None, ALU.is_gt))
                        link(nc.vector.copy_predicated(t1[:, :], mask[:, :], fills[POSINF_AS][:, :]))
                        link(nc.vector.tensor_scalar(mask[:, :], t1[:, :], -FLOAT_MAX, None, ALU.is_lt))
                        link(nc.vector.copy_predicated(t1[:, :], mask[:, :], fills[NEGINF_AS][:, :]))
                        nc.vector.tensor_tensor(y1[:, :], t1[:, :], m["x"][:, bass.ds(i, 1), :].rearrange("p a f -> p (a f)"),
                                                ALU.add).then_inc(clean_ready, 1)
                        dve.wait_ge(clean_stored, i * 16 + 16)
                with dve.Else():
                    dve.nop()

            @block.sync
            def _(sp):
                with sp.If(finite(sp) == 0):
                    with sp.Fori(0, NT - 1) as i:
                        sp.wait_ge(clean_ready, i + 1)
                        sp.dma_start(out[bass.ds(i * P, P), :], y1[:, :]).then_inc(clean_stored, 16)
                    sp.wait_ge(clean_ready, NT)
                    sp.dma_start(out[(NT - 1) * P:N, :], y1[0:s.last, :]).then_inc(clean_stored, 16)
                    sp.wait_ge(clean_stored, NT * 16)
                with sp.Else():
                    sp.nop()


_INS = ["x", "src", "dst", "edge_type_16", "edge_weight1", "L0_gnn_weight", "L0_gnn_gate_weight", "L0_ffn_gate_w",
        "L0_ffn_gate_b", "L0_ffn_w1", "L0_ffn_b1", "L0_ffn_w2", "L0_ffn_b2"]


def kernel(**inputs):
    import numpy as _np
    import concourse.bacc as _bacc
    from concourse.bass_utils import run_bass_kernel_spmd as _run

    nc = _bacc.Bacc("TRN2", target_bir_lowering=False, num_devices=1)
    arrays, args = {}, []
    for name in _INS:
        a = _np.ascontiguousarray(inputs[name])
        arrays[f"in_{name}"] = a
        args.append(nc.dram_tensor(f"in_{name}", a.shape, mybir.dt.from_np(a.dtype), kind="ExternalInput").ap())
    shape = inputs["x"].shape
    args.append(nc.dram_tensor("out_dram", shape, FP32, kind="ExternalOutput").ap())
    build(nc, *args)
    r = _run(nc, [arrays], core_ids=[0])
    return r.results[0]["out_dram"]
```

```python
import concourse.bass as bass
from concourse import mybir
from contextlib import ExitStack

FP32 = mybir.dt.float32
INT32 = mybir.dt.int32
ALU = mybir.AluOpType
ACT = mybir.ActivationFunctionType
AX = mybir.AxisListType

P = 128
BANKS = 8
BANK = 512
EPS = 1e-5
FLOAT_MAX = 3.4028234663852886e38
NAN_AS, POSINF_AS, NEGINF_AS = 0.0, 10000.0, -10000.0
GROUP = 8
SETS = 4
WINDOW = 8
PIECES = 3
EARLY = 3 * GROUP
RING = SETS * GROUP


def cdiv(a, b):
    return (a + b - 1) // b


class Shapes:

    def __init__(s, x, src, weight, w1, gate_w):
        s.N, s.D = x.shape
        s.E, = src.shape
        s.R = weight.shape[0]
        s.X = gate_w.shape[1]
        s.F = w1.shape[2]
        s.KD = s.D // P
        s.KF = s.F // P
        s.NT = cdiv(s.N, P)
        s.last = s.N - (s.NT - 1) * P
        s.T = cdiv(s.E, P)
        s.T_run = cdiv(s.T, RING) * RING
        s.EC = cdiv(s.T_run, P)
        s.T_pad = s.EC * P
        s.CAP = max(1, -(-5 * s.N // (4 * s.X)))
        s.ST = cdiv(s.CAP, P)
        s.SLOTS = s.X * s.CAP


def build(nc, x, src, dst, rel, norm, weight, gate_weight, gate_w, gate_b, w1, b1, w2, b2, out):
    s = Shapes(x, src, weight, w1, gate_w)
    N, D, R, X, F, KD, KF, NT, T = s.N, s.D, s.R, s.X, s.F, s.KD, s.KF, s.NT, s.T
    CAP, ST = s.CAP, s.ST
    with ExitStack() as ctx:
        def sb(name, shape, dt=FP32):
            return ctx.enter_context(nc.sbuf_tensor(name, shape, dt))

        def sem(name):
            return ctx.enter_context(nc.semaphore(name))

        def dram(name, shape, dt=FP32):
            return nc.dram_tensor(name, shape, dt).ap()

        m = {
            "node_table": dram("node_table", [N, D + R]),
            "message": dram("message_table", [N * R, D]),
            "span_scratch": dram("span_scratch", [6, s.T_pad]),
            "buf": dram("expert_buf", [s.SLOTS, D]),
            "ybuf": dram("expert_out", [s.SLOTS, D]),
        }
        m["x"] = sb("rows", [P, NT, D])
        m["ident"] = sb("ident", [P, P])
        m["iota"] = sb("iota", [P, P])
        m["tri"] = sb("tri", [P, P])
        m["ones"] = sb("ones", [P, P])
        m["mv"] = sb("mean_var", [P, NT, 2])
        m["rstd"] = sb("rstd", [P, NT])
        m["nmr"] = sb("std", [P, NT])
        m["slot"] = sb("slot", [P, NT], INT32)
        m["share"] = sb("share", [P, NT])
        m["banded"] = sb("banded", [1, 1], INT32)
        m["bank"] = [ctx.enter_context(nc.psum_tensor(f"bank{i}", [P, BANK], FP32)) for i in range(BANKS)]
        m["w_loaded"] = sem("w_loaded")
        m["wait_passed"] = sem("wait_passed")
        m["x_loaded"] = [sem(f"x_loaded{c}") for c in range(cdiv(NT, 7))]
        for name in ("index_ready", "group_done", "select_ready", "summed", "added"):
            m[name] = sem(name)
        m["rows_gathered"] = [sem(f"rows_gathered{i}") for i in range(RING)]
        with ExitStack() as graph:
            def gsb(name, shape, dt=FP32):
                return graph.enter_context(nc.sbuf_tensor(name, shape, dt))

            m["src_of"] = gsb("src_of", [P, s.T_pad], INT32)
            m["cols"] = gsb("edge_cols", [P, 3, s.T_pad])
            m["rel8_of"], m["norm_of"], m["key_of"] = (m["cols"][:, k, :] for k in range(3))
            m["dst_of"] = gsb("dst_of", [P, s.T_pad])
            m["group_row"] = gsb("group_row", [1, s.T_run // GROUP, 2], INT32)
            m["steer_dve"] = gsb("steer_dve", [1, s.T_run // GROUP * 3], INT32)
            m["steer_pe"] = gsb("steer_pe", [1, s.T_run // GROUP], INT32)
            m["block_base"] = gsb("block_base", [P, NT])
            m["rel_steps"] = gsb("rel_steps", [P, R])
            m["gathered"] = gsb("gathered", [P, RING, D + R])
            prepare(nc, s, m, x, src, dst, rel, norm, gate_weight)
            m["W"] = gsb("W", [P, KD, R, D])
            banded(nc, s, m, weight)
            tables(nc, s, m, gate_weight)
            edges(nc, s, m)
        routing(nc, s, m, x, gate_w, gate_b)
        experts(nc, s, m, w1, b1, w2, b2)
        combine(nc, s, m, out)


def only_if(nc, m, e, wanted, program):
    flag = nc.values_load(m["banded"][0:1, 0:1], engines=[e.engine], min_val=0, max_val=1)
    with e.If(flag == wanted):
        program(e)
    with e.Else():
        e.nop()


def prepare(nc, s, m, x, src, dst, rel, norm, gate_weight):
    N, D, R, KD, NT, T, EC = s.N, s.D, s.R, s.KD, s.NT, s.T, s.EC
    CHUNK = 7
    NCH = cdiv(NT, CHUNK)
    GROUPS = s.T_run // GROUP
    spans = [(c * CHUNK, min((c + 1) * CHUNK, NT)) for c in range(NCH)]
    with ExitStack() as ctx:
        def sb(name, shape, dt=FP32):
            return ctx.enter_context(nc.sbuf_tensor(name, shape, dt))

        def sem(name):
            return ctx.enter_context(nc.semaphore(name))

        GW_rows = sb("GW_rows", [R, D])
        GW = sb("GW", [P, KD, R])
        NODES = 4
        node = [sb(f"node_rows{i}", [P, CHUNK, D + R]) for i in range(NODES)]
        stats = sb("stats", [P, NT, 6])
        TILE_ROWS = 6
        area = sb("edge_area", [P, TILE_ROWS, s.T_pad])
        src_f, dst_f, rel_f, norm_f = (area[:, k, :].rearrange("p (j e) -> p j e", e=P) for k in range(4))
        raw = {"src": src_f.bitcast(INT32), "dst": dst_f.bitcast(INT32), "rel": rel_f.bitcast(INT32), "norm": norm_f}
        MN, B0, B1, BASE, OFF, BAD = range(TILE_ROWS)
        q = sb("tile_facts", [P, TILE_ROWS, EC])
        mx = sb("tile_max", [P, EC])
        t1 = sb("tile_t1", [P, EC])
        t2 = sb("tile_t2", [P, EC])
        ti = sb("tile_int", [P, 2, EC], INT32)
        fact = area[0:1, :, :]
        g = sb("group_facts", [1, 13, GROUPS])
        bad = sb("bad", [1, 4])
        hT = [sb(f"hT{i}", [P, KD, P]) for i in range(2)]
        bank = m["bank"]
        pT, pG, pE = bank[0:2], bank[2:4], bank[4:6]

        x_loaded = m["x_loaded"]
        x_padded = sem("x_padded")
        gw_loaded = sem("gw_loaded")
        gw_in_psum = sem("gw_in_psum")
        gw_ready = sem("gw_ready")
        edges_padded = sem("edges_padded")
        edges_loaded = sem("edges_loaded")
        consts_ready = sem("consts_ready")
        consts_step = sem("consts_step")
        dve_step = sem("dve_step")
        var_ready = sem("var_ready")
        std_ready = sem("std_ready")
        h_ready = sem("h_ready")
        hT_in_psum = sem("hT_in_psum")
        hT_ready = sem("hT_ready")
        gates_in_psum = sem("gates_in_psum")
        gates_ready = sem("gates_ready")
        nodes_stored = [sem(f"nodes_stored{c}") for c in range(NCH)]
        facts_ready = sem("facts_ready")
        facts_stored = sem("facts_stored")
        facts_loaded = sem("facts_loaded")
        cols_ready = sem("cols_ready")
        colT_in_psum = sem("colT_in_psum")
        colT_copied = sem("colT_copied")
        base_in_psum = sem("base_in_psum")
        base_used = sem("base_used")

        def stores_of(c):
            a, b = spans[c]
            return 32 if b == NT and b - a > 1 else 16

        full_tiles = s.E // P
        head = P * (EC - 1)
        EDGE_DMAS = 48 if s.E % P else 32
        NBANKS = cdiv(EC, 4)

        def place(ap, j):
            if j < EC - 1:
                return ap[:, 0:head].rearrange("e (p j) -> e j p", j=EC - 1)[:, j, :]
            return ap[:, head:head + P]

        with nc.Block() as block:
            @block.sync
            def _(sp):
                sp.dma_start(GW_rows[:, :], gate_weight.rearrange("r d o -> r (d o)")).then_inc(gw_loaded, 16)
                sp.wait_ge(edges_padded, 4)
                for name, ap in (("dst", dst), ("rel", rel), ("src", src), ("norm", norm)):
                    flat = ap if len(ap.shape) == 1 else ap.rearrange("e o -> (e o)")
                    sp.dma_start(raw[name][:, 0:EC - 1, :],
                                 flat[0:head * P].rearrange("(p j e) -> p j e", j=EC - 1, e=P)).then_inc(edges_loaded, 16)
                    n = full_tiles - head
                    sp.dma_start(raw[name][0:n, EC - 1, :],
                                 flat[head * P:full_tiles * P].rearrange("(p e) -> p e", e=P)).then_inc(edges_loaded, 16)
                    if s.E % P:
                        rest = s.E - full_tiles * P
                        sp.dma_start(raw[name][n:n + 1, EC - 1, 0:rest],
                                     flat[full_tiles * P:s.E].rearrange("(p e) -> p e", e=rest)).then_inc(edges_loaded, 16)
                sp.wait_ge(x_padded, 1)
                for c, (a, b) in enumerate(spans):
                    if b == NT:
                        b -= 1
                        sp.dma_start(m["x"][0:s.last, NT - 1, :], x[(NT - 1) * P:N, :]).then_inc(x_loaded[c], 16)
                    if b > a:
                        sp.dma_start(m["x"][:, a:b, :],
                                     x[a * P:b * P, :].rearrange("(t p) f -> p t f", p=P)).then_inc(x_loaded[c], 16)
                def facts_to_rows():
                    sp.wait_ge(facts_ready, 1)
                    sp.dma_start(m["span_scratch"][:, 0:head].rearrange("q (p j) -> p q j", j=EC - 1),
                                 q[:, :, 0:EC - 1]).then_inc(facts_stored, 16)
                    for k in range(TILE_ROWS):
                        sp.dma_start(m["span_scratch"][k, head:head + P].rearrange("(p j) -> p j", j=1),
                                     q[:, k, EC - 1:EC]).then_inc(facts_stored, 16)
                    sp.wait_ge(facts_stored, 16 * (TILE_ROWS + 1))
                    sp.dma_start(fact[0:1, :, :], m["span_scratch"].rearrange("(o q) t -> o q t", o=1)).then_inc(facts_loaded, 16)
                    sp.wait_ge(facts_loaded, 16)

                for c, (a, b) in enumerate(spans):
                    sp.wait_ge(gates_ready, c + 1)
                    sp.wait_ge(h_ready, b)
                    if b == NT:
                        b -= 1
                        sp.dma_start(m["node_table"][(NT - 1) * P:N, :],
                                     node[c % NODES][0:s.last, NT - 1 - a, :]).then_inc(nodes_stored[c], 16)
                    if b > a:
                        sp.dma_start(m["node_table"][a * P:b * P, :].rearrange("(t p) f -> p t f", p=P),
                                     node[c % NODES][:, 0:b - a, :]).then_inc(nodes_stored[c], 16)
                    if c == 0:
                        facts_to_rows()
                sp.wait_ge(facts_loaded, 16)
                for c in range(NCH):
                    sp.wait_ge(nodes_stored[c], stores_of(c))

            @block.gpsimd
            def _(pool):
                pool.memset(m["x"][:, NT - 1, :], 0.0).then_inc(x_padded, 1)
                pool.memset(m["ident"][:, :], 0.0).then_inc(consts_step, 1)
                pool.memset(m["ones"][:, :], 1.0).then_inc(consts_step, 1)
                for name, fill in (("dst", N - 1), ("rel", 0), ("src", 0), ("norm", 0.0)):
                    pool.memset(raw[name][:, EC - 1, :], fill).then_inc(edges_padded, 1)
                pool.wait_ge(consts_step, 2)
                pool.affine_select(out=m["ident"][:, :], in_=m["ident"][:, :], compare_op=ALU.not_equal, fill=1.0,
                                   base=0, pattern=[[-1, P]], channel_multiplier=1).then_inc(consts_ready, 1)
                pool.affine_select(out=m["tri"][:, :], in_=m["ones"][:, :], compare_op=ALU.is_ge, fill=0.0,
                                   base=0, pattern=[[1, P]], channel_multiplier=-1).then_inc(consts_ready, 1)
                for out, step, n in ((m["iota"], 1, P), (m["block_base"], P, NT), (m["rel_steps"], WINDOW, R)):
                    pool.iota(out[:, :], pattern=[[step, n]], base=0, channel_multiplier=0,
                              allow_small_or_imprecise_dtypes=True).then_inc(consts_ready, 1)
                pool.wait_ge(colT_copied, 3 * NBANKS)
                for c in range(NCH):
                    pool.wait_ge(nodes_stored[c], stores_of(c))
                for i in range(EARLY):
                    nc.gpsimd.indirect_dma_start(m["gathered"][:, i, :], None, m["node_table"],
                                                 bass.IndirectOffsetOnAxis(ap=m["src_of"][:, i:i + 1], axis=0)
                                                 ).then_inc(m["rows_gathered"][i], 16)

            @block.vector
            def _(dve):
                chain = [0]

                def link(ins):
                    chain[0] += 1
                    ins.then_inc(dve_step, 1)
                    dve.wait_ge(dve_step, chain[0])

                def moments(c):
                    a, b = spans[c]
                    dve.wait_ge(x_loaded[c], 16 if b < NT or b - a == 1 else 32)
                    for i in range(a, b):
                        last = nc.vector.bn_stats(stats[:, i, :], m["x"][:, i, :])
                    link(last)
                    for i in range(a, b):
                        last = nc.vector.bn_aggr(m["mv"][:, i, :], stats[:, i, :])
                    link(last)
                    nc.vector.tensor_scalar(m["nmr"][:, a:b], m["mv"][:, a:b, 1], EPS, None, ALU.add).then_inc(var_ready, 1)

                dve.wait_ge(edges_loaded, 4 * EDGE_DMAS)
                link(nc.vector.tensor_copy(dst_f, raw["dst"][:, :, :]))
                nc.vector.tensor_copy(src_f, raw["src"][:, :, :])
                nc.vector.tensor_scalar(rel_f, raw["rel"][:, :, :], float(WINDOW), None, ALU.mult).then_inc(cols_ready, 1)
                nc.vector.tensor_reduce(q[:, MN, :], dst_f, AX.X, ALU.min)
                link(nc.vector.tensor_reduce(mx[:, :], dst_f, AX.X, ALU.max))
                nc.vector.tensor_copy(ti[:, 0, :], q[:, MN, :])
                link(nc.vector.tensor_copy(ti[:, 1, :], mx[:, :]))
                link(nc.vector.tensor_scalar(ti[:, :, :], ti[:, :, :], P.bit_length() - 1, None, ALU.arith_shift_right))
                nc.vector.tensor_copy(q[:, B0, :], ti[:, 0, :])
                link(nc.vector.tensor_copy(q[:, B1, :], ti[:, 1, :]))
                link(nc.vector.tensor_scalar(t1[:, :], q[:, B0, :], float(P), float(P - WINDOW), ALU.mult, ALU.add))
                link(nc.vector.tensor_tensor(q[:, BASE, :], q[:, MN, :], t1[:, :], ALU.min))
                link(nc.vector.tensor_tensor(t1[:, :], q[:, BASE, :], t1[:, :], ALU.is_equal))
                link(nc.vector.tensor_tensor(t2[:, :], mx[:, :], q[:, BASE, :], ALU.subtract))
                link(nc.vector.tensor_scalar(t1[:, :], t1[:, :], float(WINDOW), float(WINDOW), ALU.mult, ALU.add))
                nc.vector.tensor_tensor(q[:, BAD, :], t2[:, :], t1[:, :], ALU.is_ge)
                link(nc.vector.tensor_copy(ti[:, 0, :], q[:, BASE, :]))
                link(nc.vector.tensor_scalar(ti[:, 0, :], ti[:, 0, :], 2 * P - 1, None, ALU.bitwise_and))
                nc.vector.tensor_copy(q[:, OFF, :], ti[:, 0, :])
                def order_in_tiles():
                    dve.wait_ge(colT_in_psum, 4 * NBANKS)
                    link(nc.vector.tensor_tensor(rel_f[:, :, 0:P - 1], dst_f[:, :, 0:P - 1], dst_f[:, :, 1:P], ALU.is_gt))
                    link(nc.vector.tensor_reduce(t2[:, :], rel_f[:, :, 0:P - 1], AX.X, ALU.add))
                    nc.vector.tensor_tensor(q[:, BAD, :], q[:, BAD, :], t2[:, :], ALU.add).then_inc(facts_ready, 1)

                moments(0)
                for c, (a, b) in enumerate(spans):
                    if c + 1 < NCH:
                        moments(c + 1)
                    if c == 0:
                        order_in_tiles()
                    dve.wait_ge(std_ready, c + 1)
                    link(nc.vector.reciprocal(m["rstd"][:, a:b], m["nmr"][:, a:b]))
                    if c >= NODES:
                        dve.wait_ge(nodes_stored[c - NODES], stores_of(c - NODES))
                    for i in range(a, b):
                        nc.vector.tensor_scalar(node[c % NODES][:, i - a, 0:D], m["x"][:, i, :], m["mv"][:, i, 0:1], m["rstd"][:, i:i + 1],
                                                ALU.subtract, ALU.mult).then_inc(h_ready, 1)

                dve.wait_ge(facts_loaded, 16)
                row = lambda k: fact[0:1, k, 0:s.T_run]
                by_group = lambda k: row(k).rearrange("o (g t) -> o g t", t=GROUP)
                FIRST, LAST, SUM0, NEW, TRIG, BEYOND, ODD, PACK0, PACK1, PACK2, X0, X1, NEAR = range(13)
                G = lambda k, a=0, b=GROUPS: g[0:1, k, a:b]
                nc.vector.tensor_reduce(G(FIRST), by_group(B0), AX.X, ALU.min)
                nc.vector.tensor_reduce(G(LAST), by_group(B1), AX.X, ALU.max)
                nc.vector.tensor_reduce(G(SUM0), by_group(B0), AX.X, ALU.add)
                link(nc.vector.tensor_reduce(bad[0:1, 0:1], row(BAD), AX.X, ALU.add))
                nc.vector.tensor_copy(m["group_row"][0:1, :, 0], G(FIRST))
                nc.vector.tensor_tensor(G(BEYOND), G(LAST), G(FIRST), ALU.subtract)
                nc.vector.tensor_copy(G(NEW, 0, 1), G(LAST, 0, 1))
                nc.vector.tensor_tensor(G(NEW, 1), G(LAST, 1), G(LAST, 0, GROUPS - 1), ALU.subtract)
                nc.vector.tensor_copy(G(TRIG, 0, 1), G(FIRST, 0, 1))
                nc.vector.tensor_tensor(G(TRIG, 1), G(FIRST, 1), G(FIRST, 0, GROUPS - 1), ALU.subtract)
                link(nc.vector.tensor_scalar(G(X0), G(FIRST), float(GROUP), float(GROUP - 1), ALU.mult, ALU.add))
                link(nc.vector.tensor_tensor(G(X0), G(X0), G(SUM0), ALU.subtract))
                link(nc.vector.tensor_tensor(G(X1), G(BEYOND), G(TRIG), ALU.add))
                link(nc.vector.tensor_tensor(G(X1, 1), G(X1, 1), G(TRIG, 0, GROUPS - 1), ALU.add))
                link(nc.vector.tensor_tensor(G(X1), G(X1), G(NEW), ALU.max))
                nc.vector.tensor_copy(G(NEAR, 0, 1), G(TRIG, 0, 1))
                link(nc.vector.tensor_tensor(G(NEAR, 1), G(TRIG, 1), G(TRIG, 0, GROUPS - 1), ALU.add))
                for k in range(2, PIECES):
                    link(nc.vector.tensor_tensor(G(NEAR, k), G(NEAR, k), G(TRIG, 0, GROUPS - k), ALU.add))
                link(nc.vector.tensor_tensor(G(X1), G(X1), G(NEAR), ALU.max))
                link(nc.vector.scalar_tensor_tensor(G(X1, GROUPS - PIECES + 1), G(TRIG, GROUPS - PIECES + 1), 2.0,
                                                    G(X1, GROUPS - PIECES + 1), ALU.mult, ALU.max))
                link(nc.vector.tensor_scalar(G(X1), G(X1), 1.0, None, ALU.is_gt))
                link(nc.vector.tensor_reduce(bad[0:1, 1:2], G(X1), AX.X, ALU.add))
                link(nc.vector.tensor_tensor(G(X1), G(NEW), G(TRIG), ALU.min))
                link(nc.vector.tensor_scalar(G(X1), G(X1), 0.0, None, ALU.is_lt))
                link(nc.vector.tensor_reduce(bad[0:1, 2:3], G(X1), AX.X, ALU.add))
                nc.vector.tensor_scalar(m["group_row"][0:1, :, 1], G(BEYOND), 1.0, None, ALU.add)
                nc.vector.tensor_scalar(bad[0:1, 3:4], G(FIRST, GROUPS - 1), float(NT - 1), None, ALU.not_equal)
                link(nc.vector.tensor_tensor(bad[0:1, 1:2], bad[0:1, 1:2], bad[0:1, 2:3], ALU.add))
                link(nc.vector.tensor_tensor(bad[0:1, 0:1], bad[0:1, 0:1], bad[0:1, 1:2], ALU.add))
                link(nc.vector.tensor_tensor(bad[0:1, 0:1], bad[0:1, 0:1], bad[0:1, 3:4], ALU.add))
                link(nc.vector.tensor_tensor(bad[0:1, 0:1], bad[0:1, 0:1], G(FIRST, 0, 1), ALU.add))
                nxt = fact[0:1, BAD, 0:s.T_run - 1]
                link(nc.vector.tensor_tensor(nxt, fact[0:1, MN, 0:s.T_run - 1], fact[0:1, MN, 1:s.T_run], ALU.is_gt))
                link(nc.vector.tensor_reduce(bad[0:1, 2:3], nxt, AX.X, ALU.add))
                link(nc.vector.tensor_tensor(bad[0:1, 0:1], bad[0:1, 0:1], bad[0:1, 2:3], ALU.add))
                nc.vector.tensor_scalar(m["banded"][0:1, :], bad[0:1, 0:1], 0.0, None, ALU.is_equal)
                link(nc.vector.tensor_copy(m["steer_pe"][0:1, :], G(FIRST)))
                link(nc.vector.tensor_scalar(m["steer_pe"][0:1, :], m["steer_pe"][0:1, :], 1, None, ALU.bitwise_and))
                link(nc.vector.tensor_copy(G(ODD), m["steer_pe"][0:1, :]))
                link(nc.vector.tensor_scalar(G(ODD), G(ODD), -float(PIECES), float(PIECES + 1), ALU.mult, ALU.add))
                link(nc.vector.tensor_tensor(G(ODD), G(ODD), G(TRIG), ALU.mult))
                link(nc.vector.tensor_copy(G(X1), G(ODD)))
                link(nc.vector.scalar_tensor_tensor(G(X1, 1), G(BEYOND, 0, GROUPS - 1), 8.0, G(ODD, 1), ALU.mult, ALU.add))
                for k in range(1, PIECES):
                    link(nc.vector.tensor_tensor(G(ODD), G(ODD), G(TRIG), ALU.add))
                    link(nc.vector.tensor_tensor(G(X1, k), G(X1, k), G(ODD, 0, GROUPS - k), ALU.add))
                nc.vector.tensor_copy(m["steer_pe"][0:1, :], G(X1))
                off = by_group(OFF)
                link(nc.vector.scalar_tensor_tensor(G(X0), G(BEYOND), float(GROUP), G(X0), ALU.mult, ALU.add))
                link(nc.vector.scalar_tensor_tensor(G(X0, 1), G(BEYOND, 0, GROUPS - 1), 2.0 * GROUP, G(X0, 1), ALU.mult, ALU.add))
                link(nc.vector.scalar_tensor_tensor(G(X0), G(NEW), 4.0 * GROUP, G(X0), ALU.mult, ALU.add))
                for k, parts in enumerate(((off[:, :, 2], off[:, :, 1], off[:, :, 0]), (off[:, :, 5], off[:, :, 4], off[:, :, 3]),
                                           (G(X0), off[:, :, 7], off[:, :, 6]))):
                    link(nc.vector.scalar_tensor_tensor(G(PACK0 + k), parts[0], 256.0, parts[1], ALU.mult, ALU.add))
                    link(nc.vector.scalar_tensor_tensor(G(PACK0 + k), G(PACK0 + k), 256.0, parts[2], ALU.mult, ALU.add))
                    nc.vector.tensor_copy(m["steer_dve"][0:1, :].rearrange("o (g q) -> o g q", q=3)[:, :, k], G(PACK0 + k))
                for k, c0 in enumerate(range(0, s.T_pad, BANK)):
                    c1 = min(c0 + BANK, s.T_pad)
                    key = m["key_of"][:, c0:c1]
                    dve.wait_ge(base_in_psum, k + 1)
                    nc.vector.tensor_tensor(key, m["dst_of"][:, c0:c1], pE[k % 2][:, 0:c1 - c0], ALU.subtract).then_inc(base_used, 1)
                    dve.wait_ge(base_used, k + 1)
                tmp = area[:, MN, :]
                link(nc.vector.tensor_scalar(tmp, m["key_of"][:, :], float(WINDOW), -2.0 * P, ALU.is_ge, ALU.mult))
                link(nc.vector.tensor_tensor(m["key_of"][:, :], m["key_of"][:, :], m["rel8_of"][:, :], ALU.add))
                nc.vector.tensor_tensor(m["key_of"][:, :], m["key_of"][:, :], tmp, ALU.add)

            def gates(act, c):
                a, b = spans[c]
                act.wait_ge(gates_in_psum, b)
                nc.scalar.activation(node[c % NODES][:, 0:b - a, D:D + R], pG[c % 2][:, 0:(b - a) * R].rearrange("p (t r) -> p t r", r=R),
                                     ACT.Sigmoid).then_inc(gates_ready, 1)

            @block.scalar
            def _(act):
                act.wait_ge(gw_in_psum, 1)
                nc.scalar.activation(GW[:, :, :].rearrange("p k r -> p (k r)"), pG[0][:, 0:KD * R], ACT.Copy).then_inc(gw_ready, 1)
                n = 0
                for name in ("dst_of", "rel8_of", "src_of", "norm_of"):
                    for j0 in range(0, EC, 4):
                        act.wait_ge(colT_in_psum, n + 1)
                        for j in range(j0, min(j0 + 4, EC)):
                            last = nc.scalar.activation(place(m[name], j), pE[n % 2][:, (j - j0) * P:(j - j0 + 1) * P], ACT.Copy)
                        last.then_inc(colT_copied, 1)
                        n += 1
                for c, (a, b) in enumerate(spans):
                    act.wait_ge(var_ready, c + 1)
                    nc.scalar.activation(m["nmr"][:, a:b], m["nmr"][:, a:b], ACT.Sqrt).then_inc(std_ready, 1)
                    if c:
                        gates(act, c - 1)
                    for i in range(a, b):
                        act.wait_ge(hT_in_psum, i + 1)
                        nc.scalar.activation(hT[i % 2][:, :, :].rearrange("p k n -> p (k n)"), pT[i % 2][:, 0:KD * P],
                                             ACT.Copy).then_inc(hT_ready, 1)
                gates(act, NCH - 1)

            @block.tensor
            def _(pe):
                pe.wait_ge(consts_ready, 5)
                pe.wait_ge(gw_loaded, 16)
                for k in range(KD):
                    last = nc.tensor.transpose(pG[0][:, k * R:(k + 1) * R], GW_rows[:, k * P:(k + 1) * P], m["ident"][0:R, 0:R])
                last.then_inc(gw_in_psum, 1)

                pe.wait_ge(cols_ready, 1)
                pe.wait_ge(edges_loaded, 4 * EDGE_DMAS)
                n = 0
                for of in (dst_f, rel_f, src_f, norm_f):
                    for j0 in range(0, EC, 4):
                        if n >= 2:
                            pe.wait_ge(colT_copied, n - 1)
                        for j in range(j0, min(j0 + 4, EC)):
                            last = nc.tensor.transpose(pE[n % 2][:, (j - j0) * P:(j - j0 + 1) * P], of[:, j, :], m["ident"][:, :])
                        last.then_inc(colT_in_psum, 1)
                        n += 1

                def transposes(i):
                    pe.wait_ge(h_ready, i + 1)
                    if i >= 2:
                        pe.wait_ge(hT_ready, i - 1)
                    for k in range(KD):
                        last = nc.tensor.transpose(pT[i % 2][:, k * P:(k + 1) * P], node[i // CHUNK % NODES][:, i % CHUNK, k * P:(k + 1) * P],
                                                   m["ident"][:, :])
                    last.then_inc(hT_in_psum, 1)

                transposes(0)
                pe.wait_ge(gw_ready, 1)
                for i in range(NT):
                    if i + 1 < NT:
                        transposes(i + 1)
                    c = i // CHUNK
                    if i % CHUNK == 0 and c >= 2:
                        pe.wait_ge(gates_ready, c - 1)
                    pe.wait_ge(hT_ready, i + 1)
                    for k in range(KD):
                        last = nc.tensor.matmul(pG[c % 2][:, i % CHUNK * R:(i % CHUNK + 1) * R], hT[i % 2][:, k, :], GW[:, k, :],
                                                start=k == 0, stop=k == KD - 1)
                    last.then_inc(gates_in_psum, 1)

                pe.wait_ge(colT_copied, n)
                pe.wait_ge(facts_loaded, 16)
                for k, c0 in enumerate(range(0, s.T_pad, BANK)):
                    c1 = min(c0 + BANK, s.T_pad)
                    if k >= 2:
                        pe.wait_ge(base_used, k - 1)
                    nc.tensor.matmul(pE[k % 2][:, 0:c1 - c0], m["ones"][0:1, :], fact[0:1, BASE, c0:c1],
                                     start=True, stop=True).then_inc(base_in_psum, 1)


def banded(nc, s, m, weight):
    N, D, R, KD, NT = s.N, s.D, s.R, s.KD, s.NT
    ROUNDS = s.T_run // RING
    KEYS = R * WINDOW
    assert KEYS == P
    PER_BANK = BANK // (KD * KEYS)
    with ExitStack() as ctx:
        def sb(name, shape, dt=FP32):
            return ctx.enter_context(nc.sbuf_tensor(name, shape, dt))

        def sem(name):
            return ctx.enter_context(nc.semaphore(name))

        gathered = m["gathered"]
        index = [sb(f"b_index{h}", [P, GROUP], INT32) for h in range(SETS)]
        now = [sb(f"b_cols{h}", [P, 3, GROUP]) for h in range(SETS)]
        rel_hot = sb("rel_hot", [P, GROUP, R])
        gate_hot = sb("gate_hot", [P, GROUP, R])
        gate = sb("edge_gate", [P, GROUP])
        coef = [sb(f"coef{i}", [P, GROUP]) for i in range(2)]
        select = [[sb(f"b_select{i}_{t}", [P, KEYS]) for t in range(GROUP)] for i in range(2)]
        late_rows = sb("late_rows", [P, D])
        late_key = sb("late_key", [P, 2])
        late_select = sb("late_select", [P, KEYS])
        sums = sb("sums", [P, KD, R, 2 * P])
        zero = sb("zero", [P, 1])
        CLEARS = 16
        zeros = sb("zeros", [P, s.SLOTS * D // P // CLEARS])
        visit = m["bank"][0:4]
        late = m["bank"][4]
        product = m["bank"][5:7]

        rows_gathered = m["rows_gathered"]
        index_ready = m["index_ready"]
        step_done = sem("b_step")
        hot_ready = sem("b_hot_ready")
        select_ready, tile_summed, tile_added = m["select_ready"], m["summed"], m["added"]
        group_done = m["group_done"]
        late_ready = sem("b_late_ready")
        late_step = sem("b_late_step")
        late_summed = sem("b_late_summed")
        late_added = sem("b_late_added")
        zero_ready = sem("b_zero_ready")
        half_clear = sem("b_half_clear")
        multiplied = sem("b_multiplied")
        block_out = sem("b_block_out")
        wait_passed = m["wait_passed"]
        zeros_ready = sem("zeros_ready")
        buf_cleared = sem("buf_cleared")

        def half(k):
            return sums[:, :, :, k * P:(k + 1) * P].rearrange("p k r n -> p (k r) n")

        def steer(e, table, b, width, top):
            _, values = nc.values_load_multi_w_load_instructions(
                table[0:1, bass.ds(b * (SETS * width), SETS * width)], engines=[e.engine], min_val=0, max_val=top,
                skip_runtime_bounds_check_because="prepare() makes them so")
            return [values[h * width:(h + 1) * width] for h in range(SETS)]

        with nc.Block() as block:
            @block.sync
            def _(sp):
                for k in range(KD):
                    sp.dma_start(m["W"][:, k, :, :],
                                 weight[:, k * P:(k + 1) * P, :].rearrange("r p o -> p r o")).then_inc(m["w_loaded"], 16)
                sp.wait_ge(zeros_ready, 1)
                flat = m["buf"].rearrange("s d -> (s d)").rearrange("(c p n) -> c p n", c=CLEARS, p=P)

                def clear(paced):
                    for c in range(CLEARS):
                        if paced:
                            sp.wait_ge(group_done, min(2 * c + 2, SETS * ROUNDS))
                        sp.dma_start(flat[c], zeros[:, :]).then_inc(buf_cleared, 16)

                only_if(nc, m, sp, 1, lambda sp: clear(True))
                only_if(nc, m, sp, 0, lambda sp: clear(False))
                sp.wait_ge(buf_cleared, 16 * CLEARS)

            @block.gpsimd
            def _(pool):
                def program(pool):
                    def gather_round(b):
                        for h in range(SETS):
                            pool.wait_ge(group_done, SETS * b - SETS + h + 1)
                            pool.wait_ge(index_ready, SETS * b + h + 1)
                            pool.sem_inc(wait_passed, 1)
                            for t in range(GROUP):
                                nc.gpsimd.indirect_dma_start(
                                    gathered[:, h * GROUP + t, :], None, m["node_table"],
                                    bass.IndirectOffsetOnAxis(ap=index[h][:, t:t + 1], axis=0)
                                ).then_inc(rows_gathered[h * GROUP + t], 16)

                    with pool.Fori(1, ROUNDS) as b:
                        gather_round(b)

                pool.memset(zeros[:, :], 0.0).then_inc(zeros_ready, 1)
                for i in range(EARLY, RING):
                    nc.gpsimd.indirect_dma_start(gathered[:, i, :], None, m["node_table"],
                                                 bass.IndirectOffsetOnAxis(ap=m["src_of"][:, i:i + 1], axis=0)
                                                 ).then_inc(rows_gathered[i], 16)
                only_if(nc, m, pool, 1, program)

            @block.vector
            def _(dve):
                STEPS, FIRST_STEPS = 4, 5

                def program(dve):
                    need = dve.alloc_register("b_need")
                    dve.reg_mov(need, 1)
                    at_of = [dve.alloc_register(f"b_at{i}") for i in range(2)]
                    lates = dve.alloc_register("b_dve_lates")
                    dve.reg_mov(lates, 0)

                    def fetch(g, h):
                        nc.vector.tensor_copy(now[h][:, :, :], m["cols"][:, :, bass.ds(g * GROUP, GROUP)])
                        nc.vector.tensor_copy(index[h][:, :], m["src_of"][:, bass.ds(g * GROUP, GROUP)]).then_inc(index_ready, 1)

                    def match(g, h):
                        dve.wait_ge(index_ready, g + 1)
                        nc.vector.tensor_tensor(
                            rel_hot[:, :, :], m["rel_steps"][:, :].rearrange("p (o r) -> p o r", o=1).broadcast_to([P, GROUP, R]),
                            now[h][:, 0, :].rearrange("p (t o) -> p t o", o=1).broadcast_to([P, GROUP, R]),
                            ALU.is_equal).then_inc(step_done, 1)

                    def pick(b, h, step):
                        for t in range(GROUP):
                            dve.wait_ge(rows_gathered[h * GROUP + t], 16 * b + 16)
                        dve.wait_ge(step_done, step)
                        nc.vector.tensor_tensor(gate_hot[:, :, :], rel_hot[:, :, :],
                                                gathered[:, h * GROUP:(h + 1) * GROUP, D:D + R], ALU.mult).then_inc(step_done, 1)

                    def gather_gates(step):
                        dve.wait_ge(step_done, step)
                        nc.vector.tensor_reduce(gate[:, :], gate_hot[:, :, :], AX.X, ALU.add).then_inc(step_done, 1)

                    def weigh(h, step):
                        dve.wait_ge(step_done, step)
                        nc.vector.tensor_tensor(coef[h % 2][:, :], gate[:, :], now[h][:, 1, :], ALU.mult).then_inc(step_done, 1)

                    def choose(h, t):
                        nc.vector.tensor_scalar(select[h % 2][t][:, :], m["iota"][:, :], now[h][:, 2, t:t + 1],
                                                coef[h % 2][:, t:t + 1], ALU.is_equal, ALU.mult).then_inc(select_ready, 1)

                    def add(at, bank_ap):
                        to = sums[:, :, :, bass.ds(at, WINDOW)]
                        return nc.vector.tensor_tensor(to, to, bank_ap.rearrange("p (k r n) -> p k r n", k=KD, r=R), ALU.add)

                    def between(g, b, h, t, more):
                        step = g * STEPS + FIRST_STEPS
                        following = (h + 1) % SETS
                        if t == 0:
                            pick(b + (h + 1) // SETS, following, step)
                        elif t == 1:
                            gather_gates(step + 1)
                        elif t == 2:
                            weigh(following, step + 2)
                        else:
                            if t == 3:
                                dve.wait_ge(step_done, step + 3)
                            for k in {3: (0, 1), 4: (2, 3), 5: (4, 5), 6: (6,), 7: (7,)}[t]:
                                choose(following, k)
                        if t == GROUP - 1 and more > 1:
                            match(g + 2, (h + 2) % SETS)

                    def add_group(g, b, h, packs, more=2):

                        def field(k, shift, top, why):
                            v = packs[k] >> shift if shift else packs[k]
                            return nc.s_assert_within(v & top, 0, top, skip_runtime_bounds_check_because=why)

                        new = field(2, 21, 1, "one bit")
                        dve.reg_add(need, need, new)
                        dve.wait_ge(half_clear, dve.snap(need, min_val=1, max_val=NT + 1))
                        for t in range(GROUP):
                            dve.reg_mov(at_of[t % 2], field(t // 3, 8 * (t % 3), 255, "eight bits"))
                            at = nc.s_assert_within(dve.snap(at_of[t % 2], min_val=0, max_val=255), 0, 2 * P - WINDOW,
                                                    skip_runtime_bounds_check_because="a window ends with its block at the latest")
                            if t % PER_BANK == 0:
                                dve.wait_ge(tile_summed, g * GROUP + t + PER_BANK)
                            if not (isinstance(g, int) and g == 0 and t == 0):
                                dve.wait_ge(tile_added, g * GROUP + t)
                            add(at, visit[t // PER_BANK][:, t % PER_BANK * KD * KEYS:(t % PER_BANK + 1) * KD * KEYS]).then_inc(tile_added, 1)
                            if more:
                                between(g, b, h, t, more)
                        late_now = field(2, 19, 3, "two bits")
                        with dve.If(late_now == 0):
                            dve.nop()
                        with dve.Else():
                            block_no = dve.snap(need, min_val=1, max_val=NT)
                            n = dve.snap(lates, min_val=0, max_val=NT)
                            with dve.If(late_now == 1):
                                tile = field(2, 16, GROUP - 1, "three bits")
                                col = g * GROUP + tile
                                nc.vector.tensor_copy(late_rows[:, :], gathered[:, bass.ds(tile + h * GROUP, 1), 0:D].rearrange("p a f -> p (a f)"))
                                nc.vector.tensor_tensor(late_key[:, 0:1], m["dst_of"][:, bass.ds(col, 1)],
                                                        m["block_base"][:, bass.ds(block_no - 1, 1)], ALU.subtract).then_inc(late_step, 1)
                                dve.wait_ge(late_step, n * 3 + 1)
                                nc.vector.tensor_scalar(late_key[:, 1:2], late_key[:, 0:1], 0.0, 2.0 * P, ALU.min, ALU.mult).then_inc(late_step, 1)
                                dve.wait_ge(late_step, n * 3 + 2)
                                nc.vector.scalar_tensor_tensor(late_key[:, 0:1], late_key[:, 1:2], late_key[:, 0:1],
                                                               m["rel8_of"][:, bass.ds(col, 1)], ALU.add, ALU.add).then_inc(late_step, 1)
                                dve.wait_ge(late_step, n * 3 + 3)
                                nc.vector.tensor_scalar(late_select[:, :], m["iota"][:, :], late_key[:, 0:1],
                                                        coef[h % 2][:, bass.ds(tile, 1)], ALU.is_equal, ALU.mult).then_inc(late_ready, 1)
                            with dve.Else():
                                dve.wait_ge(late_summed, n + 1)
                                dve.wait_ge(tile_added, g * GROUP + GROUP)
                                at = nc.s_assert_within(((block_no - 1) & 1) << (P.bit_length() - 1), 0, P,
                                                        skip_runtime_bounds_check_because="the start of a half")
                                add(at, late[:, 0:KD * KEYS]).then_inc(late_added, 1)
                                dve.reg_add(lates, lates, 1)
                                dve.wait_ge(late_added, n + 1)
                                dve.sem_inc(wait_passed, 1)
                            dve.nop()
                        dve.sem_inc(group_done, 1)

                    nc.vector.memset(zero[:, :], 0.0).then_inc(zero_ready, 1)
                    for h in range(SETS):
                        fetch(h, h)
                    match(0, 0)
                    pick(0, 0, 1)
                    gather_gates(2)
                    weigh(0, 3)
                    dve.wait_ge(step_done, 4)
                    for t in range(GROUP):
                        choose(0, t)
                    match(1, 1)

                    packs = steer(dve, m["steer_dve"], 0, 3, 2 ** 24 - 1)
                    for h in range(SETS):
                        add_group(h, 0, h, packs[h])
                        fetch(SETS + h, h)
                    with dve.Fori(1, ROUNDS - 1) as b:
                        packs = steer(dve, m["steer_dve"], b, 3, 2 ** 24 - 1)
                        for h in range(SETS):
                            add_group(b * SETS + h, b, h, packs[h])
                            fetch(b * SETS + SETS + h, h)
                    packs = steer(dve, m["steer_dve"], ROUNDS - 1, 3, 2 ** 24 - 1)
                    for h in range(SETS):
                        add_group((ROUNDS - 1) * SETS + h, ROUNDS - 1, h, packs[h], more=SETS - 1 - h)

                only_if(nc, m, dve, 1, program)

            @block.scalar
            def _(act):
                def program(act):
                    act.wait_ge(zero_ready, 1)
                    zeros = zero[:, 0:1].rearrange("p (a b) -> p a b", a=1).broadcast_to([P, KD * R, P])
                    for k in range(2):
                        nc.scalar.activation(half(k), zeros, ACT.Copy).then_inc(half_clear, 1)
                    act.sem_inc(block_out, 1)

                    def emit(d, k):
                        act.wait_ge(multiplied, d + 1)
                        nc.scalar.activation(half(k), zeros, ACT.Copy).then_inc(half_clear, 1)
                        nc.scalar.activation(m["x"][:, bass.ds(d, 1), :].rearrange("p a f -> p (a f)"), product[k][:, 0:D],
                                             ACT.Copy).then_inc(block_out, 1)

                    with act.Fori(0, NT // 2) as j:
                        emit(2 * j, 0)
                        emit(2 * j + 1, 1)
                    if NT % 2:
                        emit(NT - 1, 0)

                only_if(nc, m, act, 1, program)

            @block.tensor
            def _(pe):
                def program(pe):
                    blocks = pe.alloc_register("b_blocks")
                    pe.reg_mov(blocks, 0)
                    lates = pe.alloc_register("b_pe_lates")
                    pe.reg_mov(lates, 0)

                    def multiply(k, piece):
                        steps = [(r, f) for r in range(R) for f in range(KD)]
                        n = len(steps)
                        for at in range(piece * n // PIECES, (piece + 1) * n // PIECES):
                            r, f = steps[at]
                            last = nc.tensor.matmul(product[k][:, 0:D], sums[:, f, r, k * P:(k + 1) * P], m["W"][:, f, r, :],
                                                    start=at == 0, stop=at == n - 1)
                        if piece == PIECES - 1:
                            last.then_inc(multiplied, 1)

                    def sum_group(b, h, sign):
                        g = b * SETS + h
                        for t in range(GROUP):
                            bank = visit[t // PER_BANK]
                            c0 = t % PER_BANK * KD * KEYS
                            if t % PER_BANK == 0 and not (isinstance(b, int) and g == 0):
                                pe.wait_ge(tile_added, g * GROUP - GROUP + t + PER_BANK)
                            pe.wait_ge(select_ready, g * GROUP + t + 1)
                            for f in range(KD):
                                last = nc.tensor.matmul(bank[:, c0 + f * KEYS:c0 + (f + 1) * KEYS],
                                                        gathered[:, h * GROUP + t, f * P:(f + 1) * P], select[h % 2][t][:, :],
                                                        start=True, stop=True)
                            last.then_inc(tile_summed, 1)
                        with pe.If(sign < 8):
                            pe.nop()
                        with pe.Else():
                            n = pe.snap(lates, min_val=0, max_val=NT)
                            pe.wait_ge(late_ready, n + 1)
                            for f in range(KD):
                                last = nc.tensor.matmul(late[:, f * KEYS:(f + 1) * KEYS], late_rows[:, f * P:(f + 1) * P],
                                                        late_select[:, :], start=True, stop=True)
                            last.then_inc(late_summed, 1)
                            pe.reg_add(lates, lates, 1)
                        piece = nc.s_assert_within(sign & 7, 0, 2 * PIECES, skip_runtime_bounds_check_because="piece and half")

                        def choose(codes):
                            if len(codes) == 1:
                                k, p = divmod(codes[0] - 1, PIECES)
                                if p == 0:
                                    pe.wait_ge(m["w_loaded"], 16 * KD)
                                    d = pe.snap(blocks, min_val=0, max_val=NT)
                                    pe.wait_ge(tile_added, g * GROUP)
                                    pe.wait_ge(block_out, d + 1)
                                    pe.sem_inc(wait_passed, 1)
                                    pe.reg_add(blocks, blocks, 1)
                                multiply(k, p)
                                pe.nop()
                                return
                            mid = codes[len(codes) // 2]
                            with pe.If(piece < mid):
                                choose(codes[:len(codes) // 2])
                            with pe.Else():
                                choose(codes[len(codes) // 2:])
                            pe.nop()

                        if not (isinstance(b, int) and g == 0):
                            with pe.If(piece == 0):
                                pe.nop()
                            with pe.Else():
                                choose(range(1, 2 * PIECES + 1))

                    signs = steer(pe, m["steer_pe"], 0, 1, 15)
                    for h in range(SETS):
                        sum_group(0, h, signs[h][0])
                    with pe.Fori(1, ROUNDS) as b:
                        signs = steer(pe, m["steer_pe"], b, 1, 15)
                        for h in range(SETS):
                            sum_group(b, h, signs[h][0])
                    pe.wait_ge(tile_added, s.T_run)
                    pe.wait_ge(group_done, ROUNDS * SETS)
                    pe.wait_ge(block_out, NT)
                    for p in range(PIECES):
                        multiply((NT - 1) % 2, p)

                only_if(nc, m, pe, 1, program)


def tables(nc, s, m, gate_weight):
    N, D, R, KD, NT = s.N, s.D, s.R, s.KD, s.NT
    PAIR = BANK // D
    NP = R // PAIR
    with ExitStack() as ctx:
        def sb(name, shape, dt=FP32):
            return ctx.enter_context(nc.sbuf_tensor(name, shape, dt))

        def sem(name):
            return ctx.enter_context(nc.semaphore(name))

        GW_rows = sb("t_GW_rows", [R, D])
        GW = sb("t_GW", [P, KD, R])
        rows = [sb(f"table_rows{i}", [P, R, D]) for i in range(2)]
        h = sb("t_h", [P, D])
        hT = sb("t_hT", [P, KD, P])
        sg = sb("t_sg", [P, R])
        pT, pG = m["bank"][0:2]
        main = m["bank"][4:8]
        MAIN = len(main)

        gw_loaded = sem("t_gw_loaded")
        gw_in_psum = sem("t_gw_in_psum")
        gw_ready = sem("t_gw_ready")
        h_ready = sem("t_h_ready")
        hT_in_psum = sem("t_hT_in_psum")
        hT_ready = sem("t_hT_ready")
        gate_in_psum = sem("t_gate_in_psum")
        gate_ready = sem("t_gate_ready")
        pair_in_psum = sem("t_pair_in_psum")
        rows_ready = sem("t_rows_ready")
        table_stored = [sem(f"table_stored{i}") for i in range(2)]

        with nc.Block() as block:
            @block.sync
            def _(sp):
                def program(sp):
                    sp.dma_start(GW_rows[:, :], gate_weight.rearrange("r d o -> r (d o)")).then_inc(gw_loaded, 16)

                    def store(i, par, n=P):
                        sp.wait_ge(rows_ready, NP * i + NP)
                        at = i * (P * R)
                        rows_of = m["message"][bass.ds(at, P * R), :] if n == P else m["message"][at:at + n * R, :]
                        sp.dma_start(rows_of.rearrange("(p r) o -> p r o", r=R), rows[par][0:n, :, :]).then_inc(table_stored[par], 16)

                    with sp.Fori(0, (NT - 1) // 2) as j:
                        store(2 * j, 0)
                        store(2 * j + 1, 1)
                    for i in range((NT - 1) // 2 * 2, NT):
                        store(i, i % 2, P if i < NT - 1 else s.last)
                    for par in range(2):
                        sp.wait_ge(table_stored[par], 16 * len(range(par, NT, 2)))

                only_if(nc, m, sp, 0, program)

            @block.vector
            def _(dve):
                def program(dve):
                    def step(i, par):
                        nc.vector.tensor_scalar(h[:, :], m["x"][:, bass.ds(i, 1), :].rearrange("p a f -> p (a f)"),
                                                m["mv"][:, bass.ds(i, 1), 0:1].rearrange("p a f -> p (a f)"),
                                                m["rstd"][:, bass.ds(i, 1)], ALU.subtract, ALU.mult).then_inc(h_ready, 1)
                        if not (isinstance(i, int) and i < 2):
                            dve.wait_ge(table_stored[par], 16 * (i // 2) if isinstance(i, int) else 8 * i - 8 * par)
                        dve.wait_ge(gate_ready, i + 1)
                        for j in range(NP):
                            dve.wait_ge(pair_in_psum, NP * i + j + 1)
                            for q in range(PAIR):
                                r = j * PAIR + q
                                last = nc.vector.tensor_scalar(rows[par][:, r, :], main[j % MAIN][:, q * D:(q + 1) * D],
                                                               sg[:, r:r + 1], None, ALU.mult)
                            last.then_inc(rows_ready, 1)

                    step(0, 0)
                    step(1, 1)
                    with dve.Fori(1, (NT - 1) // 2) as j:
                        step(2 * j, 0)
                        step(2 * j + 1, 1)
                    for i in range((NT - 1) // 2 * 2, NT):
                        step(i, i % 2)

                only_if(nc, m, dve, 0, program)

            @block.scalar
            def _(act):
                def program(act):
                    act.wait_ge(gw_in_psum, 1)
                    nc.scalar.activation(GW[:, :, :].rearrange("p k r -> p (k r)"), pG[:, 0:KD * R], ACT.Copy).then_inc(gw_ready, 1)
                    with act.Fori(0, NT) as i:
                        act.wait_ge(hT_in_psum, i + 1)
                        nc.scalar.activation(hT[:, :, :].rearrange("p k n -> p (k n)"), pT[:, 0:KD * P], ACT.Copy).then_inc(hT_ready, 1)
                        act.wait_ge(gate_in_psum, i + 1)
                        nc.scalar.activation(sg[:, :], pG[:, 0:R], ACT.Sigmoid).then_inc(gate_ready, 1)

                only_if(nc, m, act, 0, program)

            @block.tensor
            def _(pe):
                def program(pe):
                    pe.wait_ge(gw_loaded, 16)
                    for k in range(KD):
                        last = nc.tensor.transpose(pG[:, k * R:(k + 1) * R], GW_rows[:, k * P:(k + 1) * P], m["ident"][0:R, 0:R])
                    last.then_inc(gw_in_psum, 1)
                    pe.wait_ge(gw_ready, 1)

                    def step(i, first=False):
                        pe.wait_ge(h_ready, i + 1)
                        for k in range(KD):
                            last = nc.tensor.transpose(pT[:, k * P:(k + 1) * P], h[:, k * P:(k + 1) * P], m["ident"][:, :])
                        last.then_inc(hT_in_psum, 1)
                        pe.wait_ge(hT_ready, i + 1)
                        for k in range(KD):
                            last = nc.tensor.matmul(pG[:, 0:R], hT[:, k, :], GW[:, k, :], start=k == 0, stop=k == KD - 1)
                        last.then_inc(gate_in_psum, 1)
                        for j in range(NP):
                            if not (first and j < MAIN):
                                pe.wait_ge(rows_ready, NP * i + j - (MAIN - 1))
                            for k in range(KD):
                                last = nc.tensor.matmul(main[j % MAIN][:, :], hT[:, k, :],
                                                        m["W"][:, k, j * PAIR:(j + 1) * PAIR, :].rearrange("p r o -> p (r o)"),
                                                        start=k == 0, stop=k == KD - 1)
                            last.then_inc(pair_in_psum, 1)

                    step(0, first=True)
                    with pe.Fori(1, NT) as i:
                        step(i)

                only_if(nc, m, pe, 0, program)


def edges(nc, s, m):
    N, D, R, NT = s.N, s.D, s.R, s.NT
    ROUNDS = s.T_run // RING
    with ExitStack() as ctx:
        def sb(name, shape, dt=FP32):
            return ctx.enter_context(nc.sbuf_tensor(name, shape, dt))

        def sem(name):
            return ctx.enter_context(nc.semaphore(name))

        gathered = m["gathered"]
        row_of = sb("row_of", [P, s.T_pad], INT32)
        rel_of = sb("rel_of", [P, s.T_pad])
        index = [sb(f"index{h}", [P, GROUP], INT32) for h in range(SETS)]
        shifted = sb("shifted", [P, GROUP])
        select = [sb(f"select{i}", [P, P]) for i in range(GROUP)]
        total = m["bank"][0]

        rows_gathered = m["rows_gathered"]
        rel_ready = sem("rel_ready")
        row_ready = sem("row_ready")
        index_ready = m["index_ready"]
        select_ready, visit_summed = m["select_ready"], m["summed"]
        visit_added = m["added"]
        shifted_ready = sem("shifted_ready")
        group_done = m["group_done"]
        wait_passed = m["wait_passed"]
        VISITS = s.T_run // GROUP * NT

        def span(e, g):
            _, values = nc.values_load_multi_w_load_instructions(
                m["group_row"][0:1, bass.ds(g, 1), :].rearrange("o g q -> o (g q)"),
                engines=[e.engine], min_val=0, max_val=NT)
            return values

        with nc.Block() as block:
            @block.gpsimd
            def _(pool):
                def program(pool):
                    def gather_round(b, again):
                        for h in range(SETS):
                            if again:
                                pool.wait_ge(group_done, SETS * b - SETS + h + 1)
                            pool.wait_ge(index_ready, SETS * b + h + 1)
                            pool.sem_inc(wait_passed, 1)
                            for t in range(GROUP):
                                nc.gpsimd.indirect_dma_start(
                                    gathered[:, h * GROUP + t, 0:D], None, m["message"],
                                    bass.IndirectOffsetOnAxis(ap=index[h][:, t:t + 1], axis=0)
                                ).then_inc(rows_gathered[h * GROUP + t], 16)

                    for i in range(RING):
                        pool.wait_ge(rows_gathered[i], 16)
                    gather_round(0, False)
                    with pool.Fori(1, ROUNDS) as b:
                        gather_round(b, True)

                only_if(nc, m, pool, 0, program)

            @block.vector
            def _(dve):
                def program(dve):
                    nc.vector.tensor_scalar(rel_of[:, :], m["rel8_of"][:, :], 1.0 / WINDOW, None, ALU.mult).then_inc(rel_ready, 1)
                    dve.wait_ge(rel_ready, 1)
                    nc.vector.scalar_tensor_tensor(row_of[:, :], m["src_of"][:, :], float(R), rel_of[:, :],
                                                   ALU.mult, ALU.add).then_inc(row_ready, 1)
                    dve.wait_ge(row_ready, 1)
                    nc.vector.memset(m["x"][:, :, :], 0.0).then_inc(visit_added, 1)

                    def fetch(g, h):
                        nc.vector.tensor_copy(index[h][:, :], row_of[:, bass.ds(g * GROUP, GROUP)]).then_inc(index_ready, 1)

                    visits = dve.alloc_register("dve_visits")
                    dve.reg_mov(visits, 0)

                    def visit_group(g):
                        block0, blocks = span(dve, g)
                        with dve.Fori(0, blocks) as v:
                            n = dve.snap(visits, min_val=0, max_val=VISITS)
                            at = nc.s_assert_within(block0 + v, 0, NT - 1, skip_runtime_bounds_check_because=
                                                    "block0 + blocks - 1 is the last block of the group")
                            nc.vector.tensor_scalar(shifted[:, :], m["dst_of"][:, bass.ds(g * GROUP, GROUP)],
                                                    m["block_base"][:, bass.ds(at, 1)], None,
                                                    ALU.subtract).then_inc(shifted_ready, 1)
                            dve.wait_ge(shifted_ready, n + 1)
                            for t in range(GROUP):
                                nc.vector.tensor_scalar(select[t][:, :], m["iota"][:, :], shifted[:, t:t + 1],
                                                        m["norm_of"][:, bass.ds(g * GROUP + t, 1)], ALU.is_equal, ALU.mult)
                            dve.drain().then_inc(select_ready, 1)
                            dve.wait_ge(visit_summed, n + 1)
                            dve.wait_ge(visit_added, n + 1)
                            to = m["x"][:, bass.ds(at, 1), :].rearrange("p a f -> p (a f)")
                            nc.vector.tensor_tensor(to, to, total[:, 0:D], ALU.add).then_inc(visit_added, 1)
                            dve.wait_ge(visit_added, n + 2)
                            dve.reg_add(visits, visits, 1)
                        dve.sem_inc(group_done, 1)

                    for h in range(SETS):
                        fetch(h, h)
                    with dve.Fori(0, ROUNDS - 1) as b:
                        for h in range(SETS):
                            visit_group(b * SETS + h)
                            fetch(b * SETS + SETS + h, h)
                    for h in range(SETS):
                        visit_group((ROUNDS - 1) * SETS + h)

                only_if(nc, m, dve, 0, program)

            @block.tensor
            def _(pe):
                def program(pe):
                    visits = pe.alloc_register("pe_visits")
                    pe.reg_mov(visits, 0)

                    def sum_group(b, h):
                        _, blocks = span(pe, b * SETS + h)
                        for t in range(GROUP):
                            pe.wait_ge(rows_gathered[h * GROUP + t], 16 * b + 32)
                        pe.sem_inc(wait_passed, 1)
                        with pe.Fori(0, blocks):
                            n = pe.snap(visits, min_val=0, max_val=VISITS)
                            pe.wait_ge(select_ready, n + 1)
                            for t in range(GROUP):
                                last = nc.tensor.matmul(total[:, 0:D], select[t][:, :], gathered[:, h * GROUP + t, 0:D],
                                                        start=t == 0, stop=t == GROUP - 1)
                            last.then_inc(visit_summed, 1)
                            pe.reg_add(visits, visits, 1)

                    with pe.Fori(0, ROUNDS) as b:
                        for h in range(SETS):
                            sum_group(b, h)

                only_if(nc, m, pe, 0, program)


def routing(nc, s, m, x, gate_w, gate_b):
    N, D, X, KD, NT, CAP = s.N, s.D, s.X, s.KD, s.NT, s.CAP
    CHUNK = 7
    NCH = cdiv(NT, CHUNK)
    m_slot, m_share = m["slot"], m["share"]
    with ExitStack() as ctx:
        def sb(name, shape, dt=FP32):
            return ctx.enter_context(nc.sbuf_tensor(name, shape, dt))

        def sem(name):
            return ctx.enter_context(nc.semaphore(name))

        h2 = sb("h2", [P, NT, D])
        stats = sb("stats2", [P, NT, 6])
        xr = sb("x_again", [P, NT, D])
        shift = sb("shift", [P, NT])
        hT = [sb(f"h2T{i}", [P, KD, P]) for i in range(2)]
        GW = sb("router_w", [P, KD, X])
        GB = sb("router_b", [P, X])
        L = sb("logits", [P, NT, X])
        Pe = sb("gate_exp", [P, NT, X])
        hot = sb("hot", [P, NT, X])
        tot = [sb(f"tot{i}", [P, NT, X]) for i in range(2)]
        eid = sb("expert_ids", [P, X])
        top = sb("top", [P, NT])
        den = sb("den", [P, NT])
        which = sb("which", [P, NT])
        pos = sb("pos", [P, NT])
        kept = sb("kept", [P, NT])
        slot_f = sb("slot_f", [P, NT])
        put = sb("put", [P, NT], INT32)
        token = sb("token", [P, NT])
        bank = m["bank"]
        pT = bank[0:2]
        pL, pCum, pTot = bank[2], bank[3], bank[4]

        gw_loaded = sem("router_w_loaded")
        x_padded = sem("x_again_padded")
        x_loaded = m["x_loaded"]
        ids_ready = sem("ids_ready")
        x2_ready = sem("x2_ready")
        step_done = sem("route_step")
        var_ready = sem("var2_ready")
        std_ready = sem("std2_ready")
        shift_ready = sem("shift_ready")
        h2_ready = sem("h2_ready")
        hT_in_psum = sem("h2T_in_psum")
        hT_ready = sem("h2T_ready")
        logits_in_psum = sem("logits_in_psum")
        centred = sem("centred")
        exp_ready = sem("exp_ready")
        hot_ready = sem("hot_ready")
        counts_in_psum = sem("counts_in_psum")
        put_ready = sem("put_ready")
        scattered = sem("scattered")

        with nc.Block() as block:
            @block.sync
            def _(sp):
                sp.wait_ge(x_padded, 1)
                for c in range(NCH):
                    a, b = c * CHUNK, min((c + 1) * CHUNK, NT)
                    if b == NT:
                        b -= 1
                        sp.dma_start(xr[0:s.last, NT - 1, :], x[(NT - 1) * P:N, :]).then_inc(x_loaded[c], 16)
                    if b > a:
                        sp.dma_start(xr[:, a:b, :], x[a * P:b * P, :].rearrange("(t p) f -> p t f", p=P)).then_inc(x_loaded[c], 16)
                sp.dma_start(GW[:, :, :], gate_w.rearrange("(k p) e -> p k e", p=P)).then_inc(gw_loaded, 16)
                sp.dma_start(GB[:, :], gate_b.rearrange("(o e) -> o e", o=1).broadcast_to([P, X])).then_inc(gw_loaded, 16)
                sp.wait_ge(gw_loaded, 32)

            @block.gpsimd
            def _(pool):
                pool.memset(xr[:, NT - 1, :], 0.0).then_inc(x_padded, 1)
                pool.iota(eid[:, :], pattern=[[1, X]], base=0, channel_multiplier=0,
                          allow_small_or_imprecise_dtypes=True).then_inc(ids_ready, 1)
                pool.iota(token[:, :], pattern=[[P, NT]], base=0, channel_multiplier=1,
                          allow_small_or_imprecise_dtypes=True).then_inc(ids_ready, 1)
                pool.wait_ge(put_ready, 1)
                pool.wait_ge(h2_ready, NT)
                for i in range(NT):
                    nc.gpsimd.indirect_dma_start(
                        m["buf"], bass.IndirectOffsetOnAxis(ap=put[:, i:i + 1], axis=0), h2[:, i, :], None,
                        bounds_check=s.SLOTS - 1, oob_is_err=False).then_inc(scattered, 16)
                pool.wait_ge(scattered, 16 * NT)

            @block.vector
            def _(dve):
                chain = [0]

                def link(ins):
                    chain[0] += 1
                    ins.then_inc(step_done, 1)
                    dve.wait_ge(step_done, chain[0])

                def moments(c):
                    a, b = c * CHUNK, min((c + 1) * CHUNK, NT)
                    dve.wait_ge(x_loaded[c], 2 * (16 if b < NT or b - a == 1 else 32))
                    link(nc.vector.scalar_tensor_tensor(
                        m["x"][:, a:b, :].rearrange("p t f -> p (t f)"), m["x"][:, a:b, :].rearrange("p t f -> p (t f)"), 0.0,
                        xr[:, a:b, :].rearrange("p t f -> p (t f)"), ALU.max, ALU.add))
                    for i in range(a, b):
                        last = nc.vector.bn_stats(stats[:, i, :], m["x"][:, i, :])
                    link(last)
                    for i in range(a, b):
                        last = nc.vector.bn_aggr(m["mv"][:, i, :], stats[:, i, :])
                    link(last)
                    nc.vector.tensor_scalar(m["nmr"][:, a:b], m["mv"][:, a:b, 1], EPS, None, ALU.add).then_inc(var_ready, 1)

                moments(0)
                for c in range(NCH):
                    a, b = c * CHUNK, min((c + 1) * CHUNK, NT)
                    if c + 1 < NCH:
                        moments(c + 1)
                    dve.wait_ge(std_ready, c + 1)
                    link(nc.vector.reciprocal(m["rstd"][:, a:b], m["nmr"][:, a:b]))
                    nc.vector.scalar_tensor_tensor(shift[:, a:b], m["mv"][:, a:b, 0], -1.0, m["rstd"][:, a:b],
                                                   ALU.mult, ALU.mult).then_inc(shift_ready, 1)

                def rows3(ap):
                    return ap.rearrange("p (t o) -> p t o", o=1).broadcast_to([P, NT, X])

                dve.wait_ge(gw_loaded, 32)
                dve.wait_ge(logits_in_psum, NT)
                dve.wait_ge(ids_ready, 2)
                link(nc.vector.tensor_tensor(L[:, :, :], pL[:, 0:NT * X].rearrange("p (t e) -> p t e", e=X),
                                             GB[:, :].rearrange("p (o e) -> p o e", o=1).broadcast_to([P, NT, X]), ALU.add))
                link(nc.vector.tensor_reduce(top[:, :], L[:, :, :], AX.X, ALU.max))
                nc.vector.tensor_tensor(L[:, :, :], L[:, :, :], rows3(top[:, :]), ALU.subtract).then_inc(centred, 1)
                dve.wait_ge(exp_ready, 1)
                nc.vector.tensor_reduce(den[:, :], Pe[:, :, :], AX.X, ALU.add)
                link(nc.vector.tensor_reduce(top[:, :], Pe[:, :, :], AX.X, ALU.max))
                link(nc.vector.tensor_tensor(hot[:, :, :], Pe[:, :, :], rows3(top[:, :]), ALU.is_equal))
                link(nc.vector.reciprocal(den[:, :], den[:, :]))
                nc.vector.tensor_tensor(m_share[:, :], top[:, :], den[:, :], ALU.mult)
                e3 = eid[:, :].rearrange("p (o e) -> p o e", o=1).broadcast_to([P, NT, X])
                link(nc.vector.tensor_scalar(hot[:, :, :], hot[:, :, :], -float(X), float(X), ALU.mult, ALU.add))
                link(nc.vector.tensor_tensor(hot[:, :, :], hot[:, :, :], e3, ALU.add))
                link(nc.vector.tensor_reduce(which[:, :], hot[:, :, :], AX.X, ALU.min))
                nc.vector.tensor_tensor(hot[:, :, :], e3, rows3(which[:, :]), ALU.is_equal).then_inc(hot_ready, 1)
                dve.wait_ge(counts_in_psum, 1)
                link(nc.vector.memset(tot[0][:, 0, :], 0.0))
                link(nc.vector.tensor_copy(tot[0][:, 1:NT, :], pTot[:, 0:(NT - 1) * X].rearrange("p (t e) -> p t e", e=X)))
                a, b, w = tot[0], tot[1], 1
                while w < NT:
                    nc.vector.tensor_copy(b[:, 0:w, :], a[:, 0:w, :])
                    link(nc.vector.tensor_tensor(b[:, w:NT, :], a[:, w:NT, :], a[:, 0:NT - w, :], ALU.add))
                    a, b, w = b, a, 2 * w
                link(nc.vector.tensor_tensor(b[:, :, :], a[:, :, :], pCum[:, 0:NT * X].rearrange("p (t e) -> p t e", e=X), ALU.add))
                link(nc.vector.tensor_tensor(b[:, :, :], b[:, :, :], hot[:, :, :], ALU.mult))
                link(nc.vector.tensor_reduce(pos[:, :], b[:, :, :], AX.X, ALU.add))
                link(nc.vector.tensor_scalar(pos[:, :], pos[:, :], -1.0, None, ALU.add))
                nc.vector.tensor_scalar(kept[:, :], pos[:, :], float(CAP), None, ALU.is_lt)
                nc.vector.tensor_scalar(token[:, :], token[:, :], float(N), None, ALU.is_lt)
                link(nc.vector.tensor_scalar(pos[:, :], pos[:, :], float(CAP - 1), 0.0, ALU.min, ALU.max))
                link(nc.vector.scalar_tensor_tensor(slot_f[:, :], which[:, :], float(CAP), pos[:, :], ALU.mult, ALU.add))
                nc.vector.tensor_copy(m_slot[:, :], slot_f[:, :])
                link(nc.vector.tensor_tensor(m_share[:, :], m_share[:, :], kept[:, :], ALU.mult))
                link(nc.vector.tensor_tensor(kept[:, :], kept[:, :], token[:, :], ALU.mult))
                link(nc.vector.tensor_scalar(kept[:, :], kept[:, :], -float(s.SLOTS), float(s.SLOTS), ALU.mult, ALU.add))
                link(nc.vector.tensor_tensor(slot_f[:, :], slot_f[:, :], kept[:, :], ALU.add))
                nc.vector.tensor_copy(put[:, :], slot_f[:, :]).then_inc(put_ready, 1)

            @block.scalar
            def _(act):
                def std(c):
                    a, b = c * CHUNK, min((c + 1) * CHUNK, NT)
                    act.wait_ge(var_ready, c + 1)
                    nc.scalar.activation(m["nmr"][:, a:b], m["nmr"][:, a:b], ACT.Sqrt).then_inc(std_ready, 1)

                def columns(i):
                    act.wait_ge(hT_in_psum, i + 1)
                    nc.scalar.activation(hT[i % 2][:, :, :].rearrange("p k n -> p (k n)"), pT[i % 2][:, 0:KD * P],
                                         ACT.Copy).then_inc(hT_ready, 1)

                std(0)
                for c in range(NCH):
                    if c + 1 < NCH:
                        std(c + 1)
                    act.wait_ge(shift_ready, c + 1)
                    for i in range(c * CHUNK, min((c + 1) * CHUNK, NT)):
                        nc.scalar.activation(h2[:, i, :], m["x"][:, i, :], ACT.Identity, bias=shift[:, i:i + 1],
                                             scale=m["rstd"][:, i:i + 1]).then_inc(h2_ready, 1)
                        if i:
                            columns(i - 1)
                columns(NT - 1)
                act.wait_ge(centred, 1)
                nc.scalar.activation(Pe[:, :, :].rearrange("p t e -> p (t e)"), L[:, :, :].rearrange("p t e -> p (t e)"),
                                     ACT.Exp).then_inc(exp_ready, 1)

            @block.tensor
            def _(pe):
                pe.wait_ge(gw_loaded, 32)

                def transposes(i):
                    pe.wait_ge(h2_ready, i + 1)
                    if i >= 1:
                        pe.wait_ge(hT_ready, i)
                    for k in range(KD):
                        last = nc.tensor.transpose(pT[i % 2][:, k * P:(k + 1) * P], h2[:, i, k * P:(k + 1) * P], m["ident"][:, :])
                    last.then_inc(hT_in_psum, 1)

                transposes(0)
                for i in range(NT):
                    if i + 1 < NT:
                        transposes(i + 1)
                    pe.wait_ge(hT_ready, i + 1)
                    for k in range(KD):
                        last = nc.tensor.matmul(pL[:, i * X:(i + 1) * X], hT[i % 2][:, k, :], GW[:, k, :],
                                                start=k == 0, stop=k == KD - 1)
                    last.then_inc(logits_in_psum, 1)
                pe.wait_ge(hot_ready, 1)
                flat = hot[:, :, :].rearrange("p t e -> p (t e)")
                nc.tensor.matmul(pCum[:, 0:NT * X], m["tri"][:, :], flat, start=True, stop=True)
                nc.tensor.matmul(pTot[:, 0:NT * X], m["ones"][:, :], flat, start=True, stop=True).then_inc(counts_in_psum, 1)


def experts(nc, s, m, w1, b1, w2, b2):
    D, X, F, KD, KF, CAP, ST = s.D, s.X, s.F, s.KD, s.KF, s.CAP, s.ST
    PER = BANK // P
    PARTS = cdiv(ST, PER)
    counts = [min(PER, ST - p * PER) for p in range(PARTS)]
    widths = [min(PER * P, CAP - p * PER * P) for p in range(PARTS)]
    with ExitStack() as ctx:
        def sb(name, shape, dt=FP32):
            return ctx.enter_context(nc.sbuf_tensor(name, shape, dt))

        def sem(name):
            return ctx.enter_context(nc.semaphore(name))

        W1 = [sb(f"w1_{i}", [P, KD, F]) for i in range(2)]
        W2 = [sb(f"w2_{i}", [P, KF, D]) for i in range(2)]
        B1 = sb("b1_rows", [X * KF, P])
        B1T = sb("b1_cols", [P, X * KF])
        b1_of = [sb(f"b1_of{i}", [P, KF]) for i in range(2)]
        B2 = sb("b2_all", [P, X, D])
        rows = [sb(f"slots{i}", [P, ST, D]) for i in range(2)]
        hT = [sb(f"slotsT{i}", [P, KD, PER * P]) for i in range(2)]
        mid = [sb(f"hidden{i}", [P, KF, PER * P]) for i in range(2)]
        y = [sb(f"y{i}", [P, PER, D]) for i in range(2)]
        bank = m["bank"]
        pT = bank[0:2]
        pH = bank[2:6]
        pY = bank[6:8]
        pB = bank[7]
        NH, NY = len(pH), len(pY)

        w_loaded = [sem(f"expert_w_loaded{i}") for i in range(2)]
        rows_loaded = [sem(f"slots_loaded{i}") for i in range(2)]
        b_loaded = sem("b_loaded")
        b1_in_psum = sem("b1_in_psum")
        b1_ready = sem("b1_ready")
        b1_of_ready = sem("b1_of_ready")
        T_in_psum = sem("slotsT_in_psum")
        T_ready = sem("slotsT_ready")
        hid_in_psum = sem("hidden_in_psum")
        hid_ready = sem("hidden_ready")
        y_in_psum = sem("y_in_psum")
        y_ready = sem("y_ready")
        expert_read = sem("expert_read")
        y_stored = [sem(f"y_stored{i}") for i in range(2)]
        TILES = sum(counts)
        PAIRS = X // 2

        turns = [(q, p) for q in range(2) for p in range(PARTS)]
        NTURN = len(turns)
        before = [sum(counts[p] for _, p in turns[:k]) for k in range(NTURN + 1)]

        def tile_rows(p, t):
            return min(P, CAP - (p * PER + t) * P)

        with nc.Block() as block:
            @block.sync
            def _(sp):
                sp.dma_start(B1[:, :], b1.rearrange("e (m p) -> (e m) p", p=P)).then_inc(b_loaded, 16)
                sp.dma_start(B2[:, :, :].rearrange("p e d -> p (e d)"),
                             b2.rearrange("e d -> (e d)").rearrange("(o n) -> o n", o=1).broadcast_to([P, X * D])).then_inc(b_loaded, 16)
                full = CAP // P
                rest = CAP - full * P

                def load(r, q):
                    e = 2 * r + q
                    base = e * CAP
                    sp.dma_start(rows[q][:, 0:full, :],
                                 m["buf"][bass.ds(base, full * P), :].rearrange("(t p) d -> p t d", p=P)).then_inc(rows_loaded[q], 16)
                    if rest:
                        sp.dma_start(rows[q][0:rest, full, :],
                                     m["buf"][bass.ds(base + full * P, rest), :]).then_inc(rows_loaded[q], 16)
                    sp.dma_start(W1[q][:, :, :], w1[bass.ds(e, 1), :, :].rearrange("e (k p) f -> p (e k) f", p=P)).then_inc(w_loaded[q], 16)
                    sp.dma_start(W2[q][:, :, :], w2[bass.ds(e, 1), :, :].rearrange("e (k p) d -> p (e k) d", p=P)).then_inc(w_loaded[q], 16)

                def store(r, k):
                    q, p = turns[k]
                    sp.wait_ge(y_ready, r * before[NTURN] + before[k + 1])
                    base = (2 * r + q) * CAP + p * PER * P
                    whole = counts[p] - (1 if widths[p] % P else 0)
                    if whole:
                        sp.dma_start(m["ybuf"][bass.ds(base, whole * P), :].rearrange("(t p) d -> p t d", p=P),
                                     y[k % 2][:, 0:whole, :]).then_inc(y_stored[k % 2], 16)
                    if widths[p] % P:
                        sp.dma_start(m["ybuf"][bass.ds(base + whole * P, widths[p] % P), :],
                                     y[k % 2][0:widths[p] % P, whole, :]).then_inc(y_stored[k % 2], 16)

                load(0, 0)
                load(0, 1)
                with sp.Fori(0, PAIRS - 1) as r:
                    for k, (q, p) in enumerate(turns):
                        store(r, k)
                        if p == PARTS - 1:
                            sp.wait_ge(expert_read, 2 * r + q + 1)
                            load(r + 1, q)
                for k in range(NTURN):
                    store(PAIRS - 1, k)
                for par in range(2):
                    per_round = sum(16 * ((counts[turns[k][1]] - (1 if widths[turns[k][1]] % P else 0) > 0) + (widths[turns[k][1]] % P > 0))
                                    for k in range(par, NTURN, 2))
                    sp.wait_ge(y_stored[par], PAIRS * per_round)

            def stores_before(k):
                return sum(16 * ((counts[turns[j][1]] - (1 if widths[turns[j][1]] % P else 0) > 0) + (widths[turns[j][1]] % P > 0))
                           for j in range(k % 2, k, 2))

            round_stores = [stores_before(NTURN + par) for par in range(2)]

            @block.scalar
            def _(act):
                act.wait_ge(b1_in_psum, 1)
                nc.scalar.activation(B1T[:, :], pB[:, 0:X * KF], ACT.Copy).then_inc(b1_ready, 1)
                act.wait_ge(b1_ready, 1)

                def hidden(r, k):
                    q, p = turns[k]
                    if p == 0:
                        nc.scalar.activation(b1_of[q][:, :], B1T[:, bass.ds((2 * r + q) * KF, KF)], ACT.Copy).then_inc(b1_of_ready, 1)
                        act.wait_ge(b1_of_ready, 2 * r + q + 1)
                    for f in range(KF):
                        act.wait_ge(hid_in_psum, (r * NTURN + k) * KF + f + 1)
                        nc.scalar.activation(mid[k % 2][:, f, 0:widths[p]], pH[f % NH][:, 0:widths[p]], ACT.Relu,
                                             bias=b1_of[q][:, f:f + 1]).then_inc(hid_ready, 1)

                with act.Fori(0, PAIRS) as r:
                    for k in range(NTURN):
                        hidden(r, k)

            @block.vector
            def _(dve):
                dve.wait_ge(b_loaded, 32)

                def columns(r, k):
                    q, p = turns[k]
                    dve.wait_ge(T_in_psum, r * NTURN + k + 1)
                    for f in range(KD):
                        last = nc.vector.tensor_copy(hT[k % 2][:, f, 0:widths[p]], pT[f][:, 0:widths[p]])
                    last.then_inc(T_ready, 1)

                def outputs(r, k, first=False):
                    q, p = turns[k]
                    if not (first and k < 2):
                        dve.wait_ge(y_stored[k % 2], r * round_stores[k % 2] + stores_before(k))
                    for t in range(counts[p]):
                        n = tile_rows(p, t)
                        dve.wait_ge(y_in_psum, r * before[NTURN] + before[k] + t + 1)
                        nc.vector.tensor_tensor(y[k % 2][0:n, t, :], pY[(before[k] + t) % NY][0:n, 0:D],
                                                B2[0:n, bass.ds(2 * r + q, 1), :].rearrange("p e d -> p (e d)"),
                                                ALU.add).then_inc(y_ready, 1)

                columns(0, 0)
                for k in range(NTURN):
                    columns((k + 1) // NTURN, (k + 1) % NTURN)
                    outputs(0, k, first=True)
                with dve.Fori(1, PAIRS - 1) as r:
                    for k in range(NTURN):
                        columns(r + (k + 1) // NTURN, (k + 1) % NTURN)
                        outputs(r, k)
                for k in range(NTURN):
                    if k + 1 < NTURN:
                        columns(PAIRS - 1, k + 1)
                    outputs(PAIRS - 1, k)

            @block.tensor
            def _(pe):
                pe.wait_ge(b_loaded, 32)
                nc.tensor.transpose(pB[:, 0:X * KF], B1[:, :], m["ident"][0:X * KF, 0:X * KF]).then_inc(b1_in_psum, 1)
                assert before[NTURN] % NY == 0 and KF % NH == 0

                def transposes(r, k):
                    q, p = turns[k]
                    if p == 0:
                        pe.wait_ge(rows_loaded[q], (r + 1) * (32 if CAP % P else 16))
                    if not (isinstance(r, int) and r == 0 and k == 0):
                        pe.wait_ge(T_ready, r * NTURN + k)
                    for t in range(counts[p]):
                        n = tile_rows(p, t)
                        for f in range(KD):
                            last = nc.tensor.transpose(pT[f][:, t * P:t * P + n],
                                                       rows[q][0:n, p * PER + t, f * P:(f + 1) * P], m["ident"][0:n, 0:n])
                    last.then_inc(T_in_psum, 1)

                def layer1(r, k, first):
                    q, p = turns[k]
                    pe.wait_ge(T_ready, r * NTURN + k + 1)
                    if p == 0:
                        pe.wait_ge(w_loaded[q], 32 * r + 32)
                    for f in range(KF):
                        if not (first and f < NH):
                            pe.wait_ge(hid_ready, (r * NTURN + k) * KF + f - (NH - 1))
                        for c in range(KD):
                            last = nc.tensor.matmul(pH[f % NH][:, 0:widths[p]], W1[q][:, c, f * P:(f + 1) * P],
                                                    hT[k % 2][:, c, 0:widths[p]], start=c == 0, stop=c == KD - 1)
                        last.then_inc(hid_in_psum, 1)

                def layer2(r, k, first):
                    q, p = turns[k]
                    for t in range(counts[p]):
                        n = tile_rows(p, t)
                        if not (first and t < NY):
                            pe.wait_ge(y_ready, r * before[NTURN] + before[k] + t - (NY - 1))
                        for f in range(KF):
                            if t == 0:
                                pe.wait_ge(hid_ready, (r * NTURN + k) * KF + f + 1)
                            last = nc.tensor.matmul(pY[(before[k] + t) % NY][0:n, 0:D], mid[k % 2][:, f, t * P:t * P + n],
                                                    W2[q][:, f, :], start=f == 0, stop=f == KF - 1)
                        last.then_inc(y_in_psum, 1)
                    if p == PARTS - 1:
                        pe.drain().then_inc(expert_read, 1)

                def turn(r, k, first=False, last=False):
                    if not last:
                        transposes(r + (k + 1) // NTURN, (k + 1) % NTURN)
                    layer1(r, k, first)
                    layer2(r, k, first)

                transposes(0, 0)
                for k in range(NTURN):
                    turn(0, k, first=k == 0)
                with pe.Fori(1, PAIRS - 1) as r:
                    for k in range(NTURN):
                        turn(r, k)
                for k in range(NTURN):
                    turn(PAIRS - 1, k, last=k == NTURN - 1)


def combine(nc, s, m, out):
    N, D, NT = s.N, s.D, s.NT
    RY = 8
    CHUNK = 7
    NCH = cdiv(NT, CHUNK)
    with ExitStack() as ctx:
        def sb(name, shape, dt=FP32):
            return ctx.enter_context(nc.sbuf_tensor(name, shape, dt))

        def sem(name):
            return ctx.enter_context(nc.semaphore(name))

        y = [sb(f"y_rows{i}", [P, D]) for i in range(RY)]
        res = sb("result", [P, NT, D])
        row_sum = sb("row_sum", [P, NT])
        flag = sb("flag", [P, 1])
        flag_row = sb("flag_row", [1, 1])
        flag_int = sb("flag_int", [1, 1], INT32)
        slot1 = sb("slot1", [P, 1], INT32)
        y1 = sb("clean_y", [P, D])
        t1 = sb("clean_t", [P, D])
        mask = sb("mask", [P, D], INT32)
        fills = {v: sb(f"fill{i}", [P, D]) for i, v in enumerate((NAN_AS, POSINF_AS, NEGINF_AS))}
        pF = m["bank"][0]

        gathered = [sem(f"y_gathered{i}") for i in range(RY)]
        res_ready = sem("res_ready")
        stored = sem("out_stored")
        step_done = sem("combine_step")
        flag_ready = sem("flag_ready")
        flag_in_psum = sem("flag_in_psum")
        flag_loaded = sem("flag_loaded")
        with nc.Block() as block:
            @block.gpsimd
            def _(pool):
                for i in range(NT):
                    if i >= RY:
                        pool.wait_ge(res_ready, i - RY + 1)
                    nc.gpsimd.indirect_dma_start(y[i % RY][:, :], None, m["ybuf"],
                                                 bass.IndirectOffsetOnAxis(ap=m["slot"][:, i:i + 1], axis=0)
                                                 ).then_inc(gathered[i % RY], 16)

            @block.vector
            def _(dve):
                for i in range(NT):
                    dve.wait_ge(gathered[i % RY], 16 * (i // RY + 1))
                    nc.vector.scalar_tensor_tensor(res[:, i, :], y[i % RY][:, :], m["share"][:, i:i + 1], m["x"][:, i, :],
                                                   ALU.mult, ALU.add, accum_out=row_sum[:, i:i + 1]).then_inc(res_ready, 1)
                dve.wait_ge(res_ready, NT)
                nc.vector.tensor_scalar(row_sum[:, :], row_sum[:, :], 0.0, 0.0, ALU.mult, ALU.is_equal).then_inc(step_done, 1)
                dve.wait_ge(step_done, 1)
                nc.vector.tensor_reduce(flag[:, :], row_sum[:, :], AX.X, ALU.min).then_inc(flag_ready, 1)
                dve.wait_ge(flag_in_psum, 1)
                nc.vector.tensor_reduce(flag_row[0:1, :], pF[0:1, 0:P], AX.X, ALU.min).then_inc(step_done, 1)
                dve.wait_ge(step_done, 2)
                nc.vector.tensor_copy(flag_int[0:1, :], flag_row[0:1, :]).then_inc(flag_loaded, 1)

            @block.tensor
            def _(pe):
                pe.wait_ge(flag_ready, 1)
                nc.tensor.transpose(pF[0:1, 0:P], flag[:, :], m["ident"][:, :]).then_inc(flag_in_psum, 1)

            @block.sync
            def _(sp):
                for c in range(NCH):
                    a, b = c * CHUNK, min((c + 1) * CHUNK, NT)
                    sp.wait_ge(res_ready, b)
                    if b == NT:
                        b -= 1
                        sp.dma_start(out[(NT - 1) * P:N, :], res[0:s.last, NT - 1, :]).then_inc(stored, 16)
                    if b > a:
                        sp.dma_start(out[a * P:b * P, :].rearrange("(t p) f -> p t f", p=P), res[:, a:b, :]).then_inc(stored, 16)
                sp.wait_ge(stored, 16 * (NCH + ((NT - 1) % CHUNK > 0)))
                sp.wait_ge(flag_loaded, 1)

        clean_step = sem("clean_step")
        clean_filled = sem("clean_filled")
        clean_index = sem("clean_index")
        clean_gathered = sem("clean_gathered")
        clean_ready = sem("clean_ready")
        clean_stored = sem("clean_stored")
        wait_passed = m["wait_passed"]
        with nc.Block() as block:
            def finite(e):
                return nc.values_load(flag_int[0:1, 0:1], engines=[e.engine], min_val=0, max_val=1)

            @block.gpsimd
            def _(pool):
                with pool.If(finite(pool) == 0):
                    with pool.Fori(0, NT) as i:
                        pool.wait_ge(clean_index, i + 1)
                        pool.sem_inc(wait_passed, 1)
                        nc.gpsimd.indirect_dma_start(y1[:, :], None, m["ybuf"],
                                                     bass.IndirectOffsetOnAxis(ap=slot1[:, :], axis=0)).then_inc(clean_gathered, 16)
                with pool.Else():
                    pool.nop()

            @block.vector
            def _(dve):
                with dve.If(finite(dve) == 0):
                    for v, f in fills.items():
                        nc.vector.memset(f[:, :], v).then_inc(clean_filled, 1)
                    dve.wait_ge(clean_filled, 3)
                    with dve.Fori(0, NT) as i:
                        STEPS = 7
                        count = [0]

                        def link(ins):
                            count[0] += 1
                            ins.then_inc(clean_step, 1)
                            dve.wait_ge(clean_step, i * STEPS + count[0])
                            dve.sem_inc(wait_passed, 1)

                        nc.vector.tensor_copy(slot1[:, :], m["slot"][:, bass.ds(i, 1)]).then_inc(clean_index, 1)
                        dve.wait_ge(clean_gathered, i * 16 + 16)
                        link(nc.vector.tensor_scalar(t1[:, :], y1[:, :], m["share"][:, bass.ds(i, 1)], None, ALU.mult))
                        link(nc.vector.tensor_tensor(mask[:, :], t1[:, :], t1[:, :], ALU.not_equal))
                        link(nc.vector.copy_predicated(t1[:, :], mask[:, :], fills[NAN_AS][:, :]))
                        link(nc.vector.tensor_scalar(mask[:, :], t1[:, :], FLOAT_MAX, None, ALU.is_gt))
                        link(nc.vector.copy_predicated(t1[:, :], mask[:, :], fills[POSINF_AS][:, :]))
                        link(nc.vector.tensor_scalar(mask[:, :], t1[:, :], -FLOAT_MAX, None, ALU.is_lt))
                        link(nc.vector.copy_predicated(t1[:, :], mask[:, :], fills[NEGINF_AS][:, :]))
                        nc.vector.tensor_tensor(y1[:, :], t1[:, :], m["x"][:, bass.ds(i, 1), :].rearrange("p a f -> p (a f)"),
                                                ALU.add).then_inc(clean_ready, 1)
                        dve.wait_ge(clean_stored, i * 16 + 16)
                with dve.Else():
                    dve.nop()

            @block.sync
            def _(sp):
                with sp.If(finite(sp) == 0):
                    with sp.Fori(0, NT - 1) as i:
                        sp.wait_ge(clean_ready, i + 1)
                        sp.dma_start(out[bass.ds(i * P, P), :], y1[:, :]).then_inc(clean_stored, 16)
                    sp.wait_ge(clean_ready, NT)
                    sp.dma_start(out[(NT - 1) * P:N, :], y1[0:s.last, :]).then_inc(clean_stored, 16)
                    sp.wait_ge(clean_stored, NT * 16)
                with sp.Else():
                    sp.nop()


_INS = ["x", "src", "dst", "edge_type_16", "edge_weight1", "L0_gnn_weight", "L0_gnn_gate_weight", "L0_ffn_gate_w",
        "L0_ffn_gate_b", "L0_ffn_w1", "L0_ffn_b1", "L0_ffn_w2", "L0_ffn_b2"]


def kernel(**inputs):
    import numpy as _np
    import concourse.bacc as _bacc
    from concourse.bass_utils import run_bass_kernel_spmd as _run

    nc = _bacc.Bacc("TRN2", target_bir_lowering=False, num_devices=1)
    arrays, args = {}, []
    for name in _INS:
        a = _np.ascontiguousarray(inputs[name])
        arrays[f"in_{name}"] = a
        args.append(nc.dram_tensor(f"in_{name}", a.shape, mybir.dt.from_np(a.dtype), kind="ExternalInput").ap())
    shape = inputs["x"].shape
    args.append(nc.dram_tensor("out_dram", shape, FP32, kind="ExternalOutput").ap())
    build(nc, *args)
    r = _run(nc, [arrays], core_ids=[0])
    return r.results[0]["out_dram"]
```
